# Optimizing a Trainium2 kernel written in Bass

```python
import numpy as np
import jax
import jax.numpy as jnp

def _softmax(x, axis=-1):
    return jax.nn.softmax(x, axis=axis)

def _gelu(x):
    return jax.nn.gelu(x, approximate=True)

def _silu(x):
    return jax.nn.silu(x)

def _sigmoid(x):
    return jax.nn.sigmoid(x)

def _layernorm(x, axis=-1, eps=1e-05):
    m = jnp.mean(x, axis=axis, keepdims=True)
    v = jnp.var(x, axis=axis, keepdims=True)
    return (x - m) / jnp.sqrt(v + eps)

def _scatter_add(tgt, idx, src, axis=0):
    return tgt.at[idx].add(src)

def _segment_sum(src, seg, n):
    return jax.ops.segment_sum(src, seg, n)
kernel_name = 'mk_macaron_d2_jaxref_r8_86cc9d'

def setup_inputs(seed: int=0):
    np.random.seed(seed)
    _w = jnp.asarray

    def _L0_attn_setup():
        import jax, jax.numpy as jnp
        import numpy as np
        B, S, E, H = (2, 256, 128, 16)
        key = jax.random.key(seed)
        k0, k1, k2 = jax.random.split(key, 3)
        x = jax.random.normal(k0, (B, S, E), jnp.float32)
        w_in = jax.random.normal(k1, (3 * E, E), jnp.float32) / np.sqrt(E)
        b_in = jnp.zeros((3 * E,), jnp.float32)
        w_out = jax.random.normal(k2, (E, E), jnp.float32) / np.sqrt(E)
        b_out = jnp.zeros((E,), jnp.float32)
        return {'x': x, 'w_in': w_in, 'b_in': b_in, 'w_out': w_out, 'b_out': b_out}
    _L0_attn_in = _L0_attn_setup()

    def _L0_ffn_setup():
        import jax, jax.numpy as jnp
        import numpy as np
        DIM = 128
        INTER = 64
        E = 16
        TOPK = 4
        N_GROUPS = 4
        TOPK_GROUPS = 2
        ROUTE_SCALE = 1.0
        INIT_STD = 0.02
        B, S = (2, 128)
        key = jax.random.key(seed)
        ks = jax.random.split(key, 8)
        return {'x': jax.random.normal(ks[0], (B, S, DIM), jnp.float32), 'gate_w': jax.random.normal(ks[1], (E, DIM), jnp.float32) * INIT_STD, 'gate_bias': jnp.zeros((E,), jnp.float32), 'w1': jax.random.normal(ks[2], (E, INTER, DIM), jnp.float32) * INIT_STD, 'w2': jax.random.normal(ks[3], (E, DIM, INTER), jnp.float32) * INIT_STD, 'w3': jax.random.normal(ks[4], (E, INTER, DIM), jnp.float32) * INIT_STD, 'ws1': jax.random.normal(ks[5], (INTER, DIM), jnp.float32) * INIT_STD, 'ws2': jax.random.normal(ks[6], (DIM, INTER), jnp.float32) * INIT_STD, 'ws3': jax.random.normal(ks[7], (INTER, DIM), jnp.float32) * INIT_STD}
    _L0_ffn_in = _L0_ffn_setup()

    def _L1_attn_setup():
        import jax, jax.numpy as jnp
        import numpy as np
        GROUP = 64
        MAX_REL = 32

        def _silu(x):
            return x * jax.nn.sigmoid(x)

        def _ln(x, w, b, eps=1e-05):
            m = x.mean(-1, keepdims=True)
            v = ((x - m) ** 2).mean(-1, keepdims=True)
            return (x - m) / jnp.sqrt(v + eps) * w + b

        def _rope(x):
            n, d = (x.shape[-2], x.shape[-1])
            half = d // 2
            pos = jnp.arange(n, dtype=x.dtype)
            inv_freq = 10000.0 ** (-jnp.arange(half, dtype=x.dtype) / half)
            sinusoid = pos[:, None] * inv_freq[None, :]
            sin, cos = (jnp.sin(sinusoid), jnp.cos(sinusoid))
            x1, x2 = (x[..., :half], x[..., half:])
            return jnp.concatenate([x1 * cos - x2 * sin, x2 * cos + x1 * sin], axis=-1)
        key = jax.random.key(seed)
        ks = jax.random.split(key, 8)
        B, N, D, QK, H = (4, 512, 128, 32, 256)
        s = 0.02
        return {'x': jax.random.normal(ks[0], (B, N, D), dtype=jnp.float32), 'ln1_w': jnp.ones((D,), jnp.float32), 'ln1_b': jnp.zeros((D,), jnp.float32), 'Wqk': jax.random.normal(ks[1], (QK, D), jnp.float32) * s, 'bqk': jnp.zeros((QK,), jnp.float32), 'Wv': jax.random.normal(ks[2], (H, D), jnp.float32) * s, 'bv': jnp.zeros((H,), jnp.float32), 'Wg': jax.random.normal(ks[3], (H, D), jnp.float32) * s, 'bg': jnp.zeros((H,), jnp.float32), 'Wo': jax.random.normal(ks[4], (D, H), jnp.float32) * s, 'bo': jnp.zeros((D,), jnp.float32), 'ln2_w': jnp.ones((D,), jnp.float32), 'ln2_b': jnp.zeros((D,), jnp.float32), 'gamma': jax.random.normal(ks[5], (4, QK), jnp.float32) * 0.02, 'beta': jnp.zeros((4, QK), jnp.float32), 'pos_emb': jax.random.normal(ks[6], (2 * MAX_REL + 1,), jnp.float32)}
    _L1_attn_in = _L1_attn_setup()

    def _L1_ffn_setup():
        import jax, jax.numpy as jnp
        import numpy as np
        from jax import lax
        DIM = 128
        HID = 256
        E = 8
        K = 2
        B, T = (2, 64)
        key = jax.random.key(seed)
        ks = jax.random.split(key, 5)
        scale = 1.0 / np.sqrt(DIM)
        x = jax.random.normal(ks[0], (B, T, DIM), dtype=jnp.float32)
        router_w = jax.random.normal(ks[1], (E, DIM), dtype=jnp.float32) * scale
        w_gate = jax.random.normal(ks[2], (E, HID, DIM), dtype=jnp.float32) * scale
        w_up = jax.random.normal(ks[3], (E, HID, DIM), dtype=jnp.float32) * scale
        w_down = jax.random.normal(ks[4], (E, DIM, HID), dtype=jnp.float32) * (1.0 / np.sqrt(HID))
        return {'x': x, 'router_w': router_w, 'w_gate': w_gate, 'w_up': w_up, 'w_down': w_down}
    _L1_ffn_in = _L1_ffn_setup()
    _d = {'L0_attn_x': _L0_attn_in['x'], 'L0_attn_w_in': _L0_attn_in['w_in'], 'L0_attn_b_in': _L0_attn_in['b_in'], 'L0_attn_w_out': _L0_attn_in['w_out'], 'L0_attn_b_out': _L0_attn_in['b_out'], 'L0_ffn_gate_w': _L0_ffn_in['gate_w'], 'L0_ffn_gate_bias': _L0_ffn_in['gate_bias'], 'L0_ffn_w1': _L0_ffn_in['w1'], 'L0_ffn_w2': _L0_ffn_in['w2'], 'L0_ffn_w3': _L0_ffn_in['w3'], 'L0_ffn_ws1': _L0_ffn_in['ws1'], 'L0_ffn_ws2': _L0_ffn_in['ws2'], 'L0_ffn_ws3': _L0_ffn_in['ws3'], 'L1_attn_ln1_w': _L1_attn_in['ln1_w'], 'L1_attn_ln1_b': _L1_attn_in['ln1_b'], 'L1_attn_Wqk': _L1_attn_in['Wqk'], 'L1_attn_bqk': _L1_attn_in['bqk'], 'L1_attn_Wv': _L1_attn_in['Wv'], 'L1_attn_bv': _L1_attn_in['bv'], 'L1_attn_Wg': _L1_attn_in['Wg'], 'L1_attn_bg': _L1_attn_in['bg'], 'L1_attn_Wo': _L1_attn_in['Wo'], 'L1_attn_bo': _L1_attn_in['bo'], 'L1_attn_ln2_w': _L1_attn_in['ln2_w'], 'L1_attn_ln2_b': _L1_attn_in['ln2_b'], 'L1_attn_gamma': _L1_attn_in['gamma'], 'L1_attn_beta': _L1_attn_in['beta'], 'L1_attn_pos_emb': _L1_attn_in['pos_emb'], 'L1_ffn_router_w': _L1_ffn_in['router_w'], 'L1_ffn_w_gate': _L1_ffn_in['w_gate'], 'L1_ffn_w_up': _L1_ffn_in['w_up'], 'L1_ffn_w_down': _L1_ffn_in['w_down']}
    _x0 = _d['L0_attn_x']
    _d['L0_attn_x'] = jax.random.normal(jax.random.fold_in(jax.random.key(seed), 1), (4, 1024, 128), dtype=_x0.dtype)
    del _x0
    return _d

def reference(L0_attn_x, L0_attn_w_in, L0_attn_b_in, L0_attn_w_out, L0_attn_b_out, L0_ffn_gate_w, L0_ffn_gate_bias, L0_ffn_w1, L0_ffn_w2, L0_ffn_w3, L0_ffn_ws1, L0_ffn_ws2, L0_ffn_ws3, L1_attn_ln1_w, L1_attn_ln1_b, L1_attn_Wqk, L1_attn_bqk, L1_attn_Wv, L1_attn_bv, L1_attn_Wg, L1_attn_bg, L1_attn_Wo, L1_attn_bo, L1_attn_ln2_w, L1_attn_ln2_b, L1_attn_gamma, L1_attn_beta, L1_attn_pos_emb, L1_ffn_router_w, L1_ffn_w_gate, L1_ffn_w_up, L1_ffn_w_down):

    def _L0_attn_ref(x, w_in, b_in, w_out, b_out):
        import jax, jax.numpy as jnp
        import numpy as np
        B, S, E, H = (2, 256, 128, 16)
        bsz, slen, esz = x.shape
        hsz = esz // H
        qkv = x @ w_in.T + b_in
        q, k, v = jnp.split(qkv, 3, axis=-1)

        def to_heads(t):
            return t.reshape(bsz, slen, H, hsz).transpose(0, 2, 1, 3)
        q, k, v = (to_heads(q), to_heads(k), to_heads(v))
        scale = np.float32(1.0 / np.sqrt(hsz))
        scores = jnp.einsum('bhqd,bhkd->bhqk', q * scale, k)
        causal_bias = jnp.where(jnp.tril(jnp.ones((slen, slen), dtype=bool)), 0.0, -jnp.inf).astype(x.dtype)
        scores = scores + causal_bias
        attn = jax.nn.softmax(scores, axis=-1)
        out = jnp.einsum('bhqk,bhkd->bhqd', attn, v)
        out = out.transpose(0, 2, 1, 3).reshape(bsz, slen, esz)
        out = out @ w_out.T + b_out
        out = jnp.where(jnp.isnan(out), jnp.zeros((), out.dtype), out)
        return out

    def _L0_ffn_ref(x, gate_w, gate_bias, w1, w2, w3, ws1, ws2, ws3):
        import jax, jax.numpy as jnp
        import numpy as np
        DIM = 128
        INTER = 64
        E = 16
        TOPK = 4
        N_GROUPS = 4
        TOPK_GROUPS = 2
        ROUTE_SCALE = 1.0
        INIT_STD = 0.02
        B, S = (2, 128)
        Bx, Sx, D = x.shape
        T = Bx * Sx
        xf = x.reshape(T, D)
        scores = jax.nn.sigmoid(xf @ gate_w.T)
        original_scores = scores
        s = scores + gate_bias
        sg = s.reshape(T, N_GROUPS, E // N_GROUPS)
        group_scores = sg.max(axis=-1)
        _, gidx = jax.lax.top_k(group_scores, TOPK_GROUPS)
        keep = jnp.zeros((T, N_GROUPS), bool).at[jnp.arange(T)[:, None], gidx].set(True)
        s_masked = jnp.where(keep[:, :, None], sg, -jnp.inf).reshape(T, E)
        _, idx = jax.lax.top_k(s_masked, TOPK)
        weights = jnp.take_along_axis(original_scores, idx, axis=1) * ROUTE_SCALE
        comb = jnp.zeros((T, E), x.dtype).at[jnp.arange(T)[:, None], idx].add(weights)
        h1 = jnp.einsum('td,eid->tei', xf, w1)
        h3 = jnp.einsum('td,eid->tei', xf, w3)
        h = jax.nn.silu(h1) * h3
        y = jnp.einsum('tei,edi,te->td', h, w2, comb)
        z = jax.nn.silu(xf @ ws1.T) * (xf @ ws3.T) @ ws2.T
        return (y + z).reshape(Bx, Sx, D)

    def _L1_attn_ref(x, ln1_w, ln1_b, Wqk, bqk, Wv, bv, Wg, bg, Wo, bo, ln2_w, ln2_b, gamma, beta, pos_emb):
        import jax, jax.numpy as jnp
        import numpy as np
        GROUP = 64
        MAX_REL = 32

        def _silu(x):
            return x * jax.nn.sigmoid(x)

        def _ln(x, w, b, eps=1e-05):
            m = x.mean(-1, keepdims=True)
            v = ((x - m) ** 2).mean(-1, keepdims=True)
            return (x - m) / jnp.sqrt(v + eps) * w + b

        def _rope(x):
            n, d = (x.shape[-2], x.shape[-1])
            half = d // 2
            pos = jnp.arange(n, dtype=x.dtype)
            inv_freq = 10000.0 ** (-jnp.arange(half, dtype=x.dtype) / half)
            sinusoid = pos[:, None] * inv_freq[None, :]
            sin, cos = (jnp.sin(sinusoid), jnp.cos(sinusoid))
            x1, x2 = (x[..., :half], x[..., half:])
            return jnp.concatenate([x1 * cos - x2 * sin, x2 * cos + x1 * sin], axis=-1)
        b, n, d = x.shape
        G = GROUP
        x = _ln(x, ln1_w, ln1_b)
        qk = _silu(x @ Wqk.T + bqk)
        v = _silu(x @ Wv.T + bv)
        heads = qk[..., None, :] * gamma + beta
        quad_q, lin_q, quad_k, lin_k = (heads[..., i, :] for i in range(4))
        quad_q, lin_q, quad_k, lin_k = map(_rope, (quad_q, lin_q, quad_k, lin_k))
        g = n // G
        rs = lambda t: t.reshape(b, g, G, t.shape[-1])
        qq, lq, qkk, lk, vg = map(rs, (quad_q, lin_q, quad_k, lin_k, v))
        idx = jnp.arange(G)
        dist = jnp.clip(jnp.abs(idx[:, None] - idx[None, :]), 0, MAX_REL)
        bias = pos_emb[dist]
        quad_att = jnp.einsum('bgid,bgjd->bgij', qq, qkk) / G + bias
        attn = jax.nn.relu(quad_att) ** 2
        quad_out = jnp.einsum('bgij,bgje->bgie', attn, vg)
        lin_kv = jnp.einsum('bgnd,bgne->bde', lk, vg) / n
        lin_out = jnp.einsum('bgnd,bde->bgne', lq, lin_kv)
        qo = quad_out.reshape(b, n, -1)
        lo = lin_out.reshape(b, n, -1)
        gate = _silu(x @ Wg.T + bg)
        out = gate * (qo + lo)
        out = out @ Wo.T + bo
        return _ln(out, ln2_w, ln2_b)

    def _L1_ffn_ref(x, router_w, w_gate, w_up, w_down):
        import jax, jax.numpy as jnp
        import numpy as np
        from jax import lax
        DIM = 128
        HID = 256
        E = 8
        K = 2
        B, T = (2, 64)
        Bb, Tt, D = x.shape
        N = Bb * Tt
        xf = x.reshape(N, D)
        logits = xf @ router_w.T
        routing = jax.nn.softmax(logits, axis=-1)
        top_w, top_i = lax.top_k(routing, K)
        top_w = top_w / jnp.sum(top_w, axis=-1, keepdims=True)
        combine = jnp.zeros((N, E), dtype=x.dtype)
        combine = combine.at[jnp.arange(N)[:, None], top_i].add(top_w)
        g = jnp.einsum('nd,ehd->neh', xf, w_gate)
        u = jnp.einsum('nd,ehd->neh', xf, w_up)
        h = jax.nn.silu(g) * u
        y = jnp.einsum('neh,edh->ned', h, w_down)
        out = jnp.einsum('ned,ne->nd', y, combine)
        return out.reshape(Bb, Tt, D)
    x = L0_attn_x
    x = x + 0.5 * _L0_ffn_ref(_layernorm(x, axis=-1), L0_ffn_gate_w, L0_ffn_gate_bias, L0_ffn_w1, L0_ffn_w2, L0_ffn_w3, L0_ffn_ws1, L0_ffn_ws2, L0_ffn_ws3)
    x = x + _L0_attn_ref(_layernorm(x, axis=-1), L0_attn_w_in, L0_attn_b_in, L0_attn_w_out, L0_attn_b_out)
    x = x + 0.5 * _L0_ffn_ref(_layernorm(x, axis=-1), L0_ffn_gate_w, L0_ffn_gate_bias, L0_ffn_w1, L0_ffn_w2, L0_ffn_w3, L0_ffn_ws1, L0_ffn_ws2, L0_ffn_ws3)
    x = x + 0.5 * _L1_ffn_ref(_layernorm(x, axis=-1), L1_ffn_router_w, L1_ffn_w_gate, L1_ffn_w_up, L1_ffn_w_down)
    x = x + _L1_attn_ref(_layernorm(x, axis=-1), L1_attn_ln1_w, L1_attn_ln1_b, L1_attn_Wqk, L1_attn_bqk, L1_attn_Wv, L1_attn_bv, L1_attn_Wg, L1_attn_bg, L1_attn_Wo, L1_attn_bo, L1_attn_ln2_w, L1_attn_ln2_b, L1_attn_gamma, L1_attn_beta, L1_attn_pos_emb)
    x = x + 0.5 * _L1_ffn_ref(_layernorm(x, axis=-1), L1_ffn_router_w, L1_ffn_w_gate, L1_ffn_w_up, L1_ffn_w_down)
    return x

_drawn_inputs = setup_inputs


def setup_inputs(seed=0):
    import zlib

    import numpy as np

    out = dict(_drawn_inputs(seed))
    spreads = {'L0_attn_b_in': (0.0, 0.1),
     'L0_attn_b_out': (0.0, 0.1),
     'L0_ffn_gate_bias': (0.0, 0.784),
     'L1_attn_ln1_w': (1.0, 0.2),
     'L1_attn_ln1_b': (0.0, 0.1),
     'L1_attn_bqk': (0.0, 2.0),
     'L1_attn_bv': (0.0, 0.1),
     'L1_attn_bg': (0.0, 0.1),
     'L1_attn_bo': (0.0, 0.1),
     'L1_attn_ln2_w': (1.0, 0.2),
     'L1_attn_ln2_b': (0.0, 0.1),
     'L1_attn_beta': (0.0, 2.0)}
    factors = {'L0_ffn_gate_w': 7.155,
     'L0_ffn_w1': 5.444,
     'L0_ffn_w2': 5.276,
     'L0_ffn_w3': 5.523,
     'L0_ffn_ws1': 6.043,
     'L0_ffn_ws2': 6.331,
     'L0_ffn_ws3': 6.026,
     'L1_attn_Wqk': 46.904,
     'L1_attn_gamma': 43.523}
    for name, (base, spread) in spreads.items():
        noise = np.random.default_rng([zlib.crc32(name.encode()), seed]).standard_normal(out[name].shape)
        drawn = base * np.exp(spread * noise) if base else spread * noise
        out[name] = jnp.asarray(drawn.astype(out[name].dtype))
    for name, factor in factors.items():
        out[name] = (out[name] * factor).astype(out[name].dtype)
    return out
```

```python
from contextlib import ExitStack

import numpy as np
import concourse.bass as bass
from concourse import mybir

F32 = mybir.dt.float32
F32R = mybir.dt.float32r
BF16 = mybir.dt.bfloat16
ALU = mybir.AluOpType
ACT = mybir.ActivationFunctionType
AX = mybir.AxisListType

P = 128
D = 128
B, S = 4, 1024
T = B * S
NT = T // P
G = 512
NG = T // G
TG = G // P
EPS = 1e-5

E0, I0 = 16, 64
C0 = (E0 + 2) * I0 // P
E1, I1 = 8, 256
C1 = E1 * I1 // P

H, DH = 16, 8
HG = 4
SPAN = 64
QK, HV = 32, 256
NPOS = 33

PAD = -2e30
OUT = -1e30
TAKEN = -3e30


def pack_layout():
    at, lay = 0, {}
    for name, n in (("ident", P), ("causal", P), ("causalT", P), ("qsign", 1), ("qlow", 1), ("ksign", 1),
                    ("klow", 1), ("dist", P), ("outside", P), ("sel0", C0 * P), ("sel1", E1 * P),
                    ("dval", NPOS), ("cos", S), ("sin", S)):
        lay[name] = (at, at + n)
        at += n
    return lay, at


def constants():
    lay, n = pack_layout()
    c = np.zeros((P, n), np.float32)

    def put(name):
        a, b = lay[name]
        return c[:, a:b]

    put("ident")[:] = np.eye(P)
    s0, s1 = put("sel0"), put("sel1")
    for m in range(C0 * P):
        e = m // I0
        if e <= E0:
            s0[e, m] = s0[32 + e, m] = 1
    for e in range(E1):
        s1[e, e * P:(e + 1) * P] = s1[32 + e, e * P:(e + 1) * P] = 1
    i = np.arange(P)
    put("causal")[:] = np.where(i[None, :] > i[:, None], OUT, 0)
    put("causalT")[:] = np.where(i[:, None] > i[None, :], OUT, 0)
    r = i % 32
    qlow, klow = (r >= 8) & (r < 16), (r >= 16) & (r < 24)
    put("qlow")[:, 0], put("klow")[:, 0] = qlow, klow
    put("qsign")[:, 0], put("ksign")[:, 0] = 1 - 2 * qlow, 1 - 2 * klow
    same = (i[:, None] // SPAN) == (i[None, :] // SPAN)
    put("dist")[:] = np.where(same, np.minimum(np.abs(i[:, None] - i[None, :]), NPOS - 1), -1)
    put("outside")[:] = np.where(same, 0, OUT)
    put("dval")[:] = np.arange(NPOS)
    half = QK // 2
    inv = (np.float32(10000.0) ** (-np.arange(half, dtype=np.float32) / np.float32(half))).astype(np.float32)
    ang = np.arange(S, dtype=np.float32)[None, :] * inv[:, None]
    put("cos")[:] = np.tile(np.cos(ang), (P // half, 1))
    put("sin")[:] = np.tile(np.concatenate([-np.sin(ang), np.sin(ang)]), (P // QK, 1))
    return c


def pause(dve, k):
    dve.memset(k.unread[:], 0.0)


class Core:
    pass


def phase_setup(nc, k, a, layer):
    first = layer == 0
    NC, NSEL = (C0, C0) if first else (C1, E1)
    lay, npack = pack_layout()
    with ExitStack() as ctx:
        def sb(name, shape, dt=F32):
            return ctx.enter_context(nc.sbuf_tensor(f"{name}{layer}", shape, dt))

        def sem(name):
            return ctx.enter_context(nc.semaphore(name))

        raw = sb("raw", [P, 3, NC * P])
        sel_raw = sb("sel_raw", [P, NSEL * P])
        router_raw = sb("router_raw", [P, P])
        turn = k.banks[:, 0:4, :]

        def sem(name):
            return ctx.enter_context(nc.semaphore(f"setup{layer}_{name}"))

        consts_in, x_in, cleared, small_in = sem("consts_in"), sem("x_in"), sem("cleared"), sem("small_in")
        w_in = [sem(f"w_in{n}") for n in range(3)]
        turned, high_done, low_done = sem("turned"), sem("high_done"), sem("low_done")

        jobs = []
        for w, dst in ((0, (k.wgh, k.wgl)), (1, (k.wuh, k.wul)), (2, (k.wdt, None))):
            for c in range(0, NC, 4):
                jobs.append((w, c, min(4, NC - c), dst))
        lows = [n for n, job in enumerate(jobs) if job[3][1] is not None]
        N = len(jobs)

        block = ctx.enter_context(nc.Block())

        @block.sync
        def _(sp):
            if first:
                sp.dma_start(k.pack[:], a["consts"][:, 0:k.pack.shape[1]]).then_inc(consts_in, 16)
            sp.dma_start(sel_raw[:], a["consts"][:, slice(*lay["sel0" if first else "sel1"])]).then_inc(consts_in, 16)
            sp.wait_ge(cleared, 1)
            if first:
                for w, name in ((0, "w1"), (1, "w3")):
                    sp.dma_start(raw[:, w, 0:8 * P].rearrange("p (c d) -> p c d", d=D),
                                 a["L0_ffn_" + name].rearrange("(c e) i d -> (e i) c d", e=2)).then_inc(w_in[w], 16)
                    sp.dma_start(raw[0:I0, w, 8 * P:9 * P], a["L0_ffn_ws" + name[1]]).then_inc(w_in[w], 16)
                sp.dma_start(raw[:, 2, 0:8 * P].rearrange("p (e i) -> p e i", i=I0),
                             a["L0_ffn_w2"].rearrange("e d i -> d e i")).then_inc(w_in[2], 16)
                sp.dma_start(raw[:, 2, 8 * P:8 * P + I0], a["L0_ffn_ws2"]).then_inc(w_in[2], 16)
            else:
                for w, name in ((0, "w_gate"), (1, "w_up")):
                    sp.dma_start(raw[:, w, :].rearrange("p (c d) -> p c d", d=D),
                                 a["L1_ffn_" + name].rearrange("e (c p) d -> p (e c) d", p=P)).then_inc(w_in[w], 16)
                sp.dma_start(raw[:, 2, :].rearrange("p (e i) -> p e i", i=I1),
                             a["L1_ffn_w_down"].rearrange("e d i -> d e i")).then_inc(w_in[2], 16)

        @block.scalar
        def _(act):
            if first:
                act.dma_start(k.x[:].rearrange("p (n d) -> p n d", d=D),
                              a["L0_attn_x"].rearrange("b (n p) d -> p (b n) d", p=P)).then_inc(x_in, 16)
            for n, (_, c, m, (high, _)) in enumerate(jobs):
                act.wait_ge(turned, n + 1)
                act.activation(high[:, c * P:(c + m) * P], turn[:, n % 4, 0:m * P], ACT.Copy).then_inc(high_done, 1)
            act.wait_ge(turned, N + 1)
            act.activation(k.rth[:], turn[:, N % 4, 0:P], ACT.Copy).then_inc(high_done, 1)
            if first:
                act.wait_ge(x_in, 16)

        @block.gpsimd
        def _(pool):
            pool.memset(router_raw[:], 0.0)
            if first:
                pool.memset(raw[:, :, 8 * P:9 * P], 0.0)
            pool.memset(k.neghalf[:], -0.5).then_inc(cleared, 1)
            pool.wait_ge(cleared, 1)
            router = a["L0_ffn_gate_w" if first else "L1_ffn_router_w"]
            pool.dma_start(router_raw[0:router.shape[0], :], router).then_inc(small_in, 16)
            pool.dma_start(k.gate_bias[:], a["L0_ffn_gate_bias"].partition_broadcast(P)).then_inc(small_in, 16)

        @block.tensor
        def _(pe):
            pe.wait_ge(consts_in, 32 if first else 16)
            for n, (w, c, m, _) in enumerate(jobs):
                pe.wait_ge(w_in[w], 32 if first else 16)
                if n >= 4:
                    pe.wait_ge(high_done, n - 3)
                    if n - 4 in lows:
                        pe.wait_ge(low_done, lows.index(n - 4) + 1)
                for j in range(m):
                    mm = pe.transpose(turn[:, n % 4, j * P:(j + 1) * P], raw[:, w, (c + j) * P:(c + j + 1) * P],
                                      k.ident)
                mm.then_inc(turned, 1)
            pe.wait_ge(small_in, 32)
            pe.wait_ge(high_done, N - 3)
            pe.wait_ge(low_done, len(lows) if N - 4 in lows else 1)
            pe.transpose(turn[:, N % 4, 0:P], router_raw[:], k.ident).then_inc(turned, 1)

        @block.vector
        def _(dve):
            for n, (_, c, m, (high, low)) in enumerate(jobs):
                if low is not None:
                    dve.wait_ge(high_done, n + 1)
                    dve.tensor_tensor(low[:, c * P:(c + m) * P], turn[:, n % 4, 0:m * P],
                                      high[:, c * P:(c + m) * P].bitcast(F32), ALU.subtract).then_inc(low_done, 1)
            dve.wait_ge(consts_in, 32 if first else 16)
            dve.tensor_copy(k.sel[:], sel_raw[:])
            dve.wait_ge(high_done, N + 1)
            dve.tensor_tensor(k.rtl[:], turn[:, N % 4, 0:P], k.rth[:].bitcast(F32), ALU.subtract)


def phase_moe(nc, k, tag, layer, turn_no):
    first = layer == 0
    NC = C0 if first else C1
    NE = E0 if first else E1
    gate_h, gate_l, up_h, up_l, down, sel = k.wgh, k.wgl, k.wuh, k.wul, k.wdt, k.sel

    def selector(c):
        c = c if first else c // (I1 // P)
        return sel[:, c * P:(c + 1) * P]

    g0 = turn_no * NG

    def rows(g):
        return (g - g0) * G

    with ExitStack() as ctx:
        def sem(name):
            if name not in k.moe_sems:
                k.moe_sems[name] = k.for_layer(nc.semaphore(f"moe{layer}_{name}"))
            return k.moe_sems[name]

        def sb(name, shape, dt=F32):
            return ctx.enter_context(nc.sbuf_tensor(f"{tag}_{name}", shape, dt))

        st, mv, veps, rstd = sb("st", [P, TG, 6]), sb("mv", [P, TG, 2]), sb("veps", [P, TG]), sb("rstd", [P, TG])
        xn, xh_sb, xl_sb = sb("xn", [P, TG, D]), sb("xh", [P, 2, G], F32R), sb("xl", [P, 2, G], F32R)
        logits, th, sig, comb = (sb("logits", [P, G]), sb("th", [P, TG, NE]), sb("sig", [P, TG, NE]),
                                 sb("comb", [P, TG, NE]))
        ext, mark = sb("ext", [P, TG, NE + 8]), sb("mark", [P, TG, NE + 8])
        gext, gmark = sb("gext", [P, TG, 12]), sb("gmark", [P, TG, 12])
        top_sb, pen, hs, df = (sb("top", [P, TG, 8]), sb("pen", [P, TG, 4]), sb("hs", [P, TG, 1]),
                               sb("df", [P, TG, E1]))
        cstack, combt = sb("cstack", [P, TG, P]), sb("combt", [P, 2, G], F32R)
        sil, scl, hid = sb("sil", [P, 2, G]), sb("scl", [P, 2, G]), sb("hid", [P, 2, G])

        gate_ps, up_ps, comb_ps = k.banks[:, 0:2, :], k.banks[:, 2:4, :], k.banks[:, 4:6, :]
        y_ps, misc = k.banks[:, 6, :], k.banks[:, 7, :]
        misc3 = misc[:].rearrange("p (t c) -> p t c", c=P)

        stats_done, aggr_done, eps_done, rstd_done, norm_done = (sem(s) for s in
            ("stats_done", "aggr_done", "eps_done", "rstd_done", "norm_done"))
        xt_turned, xh_done, xl_done = sem("xt_turned"), sem("xh_done"), sem("xl_done")
        logits_t, logits_out, logits_turned, logits_read = (sem(s) for s in
            ("logits_t", "logits_out", "logits_turned", "logits_read"))
        route = sem("route")
        tanh_done = sem("tanh_done")
        comb_turned, comb_t = sem("comb_turned"), sem("comb_t")
        y_done, y_added = sem("y_done"), sem("y_added")
        gate_done, up_done, silu_done, scaled, hidden, down_done = (sem(s) for s in
            ("gate_done", "up_done", "silu_done", "scaled", "hidden", "down_done"))
        comb_done, comb_high, stack_cleared = sem("comb_done"), sem("comb_high"), sem("stack_cleared")
        ROUTE = 12 if first else 8

        if first:
            slot = dict(stats=0, aggr=0, rstd=0, norm=1, turn=2, xh=2, xl=2, logit=3, lout=3, lturn=4,
                        r1=4, r2=5, r3=6, r4=7, cturn=8, y=1)
        else:
            slot = dict(stats=0, aggr=0, rstd=0, norm=2, turn=3, xh=3, xl=3, logit=5, lout=5, lturn=7,
                        r1=7, r2=9, r3=11, r4=13, cturn=14, y=1)

        block = ctx.enter_context(nc.Block())

        @block.tensor
        def _(pe):
            def turn(g, q):
                pe.wait_ge(norm_done, g + 1)
                if not isinstance(g, int) or g > 0:
                    pe.wait_ge(comb_t, g)
                for t in range(TG):
                    mm = pe.transpose(misc[:, t * P:(t + 1) * P], xn[:, t, :], k.ident)
                mm.then_inc(xt_turned, 1)

            def logit(g, q):
                pe.wait_ge(xl_done, g + 1)
                pe.matmul(misc[:], k.rth[:], xh_sb[:, q, :], start=True, stop=False)
                pe.matmul(misc[:], k.rth[:], xl_sb[:, q, :], start=False, stop=False)
                pe.matmul(misc[:], k.rtl[:], xh_sb[:, q, :], start=False, stop=True).then_inc(logits_t, 1)

            def lturn(g, q):
                pe.wait_ge(logits_out, g + 1)
                for t in range(TG):
                    mm = pe.transpose(misc[:, t * P:(t + 1) * P], logits[:, t * P:(t + 1) * P], k.ident)
                mm.then_inc(logits_turned, 1)

            def cturn(g, q):
                pe.wait_ge(route, (g + 1) * ROUTE)
                for t in range(TG):
                    mm = pe.transpose(misc[:, t * P:(t + 1) * P], cstack[:, t, :], k.ident)
                mm.then_inc(comb_turned, 1)

            def up_and_gate(g, q, c):
                n = (q * NC + c) % 2
                num = g * NC + c
                if c == 0:
                    pe.wait_ge(comb_t, g + 1)
                if not (isinstance(num, int) and num < 2):
                    pe.wait_ge(silu_done, num - 1)
                ws = slice(c * P, (c + 1) * P)
                for m, (w, xx) in enumerate(((gate_h, xh_sb), (gate_h, xl_sb), (gate_l, xh_sb))):
                    mm = pe.matmul(gate_ps[:, n, :], w[:, ws], xx[:, q, :], start=m == 0, stop=m == 2)
                mm.then_inc(gate_done, 1)
                if not (isinstance(num, int) and num < 2):
                    pe.wait_ge(hidden, num - 1)
                pe.matmul(comb_ps[:, n, :], selector(c), combt[:, q, :], start=True, stop=True)
                for m, (w, xx) in enumerate(((up_h, xh_sb), (up_h, xl_sb), (up_l, xh_sb))):
                    mm = pe.matmul(up_ps[:, n, :], w[:, ws], xx[:, q, :], start=m == 0, stop=m == 2)
                mm.then_inc(up_done, 1)

            def project(g, q, c):
                n = (q * NC + c) % 2
                pe.wait_ge(hidden, g * NC + c + 1)
                if c == 0 and not (isinstance(g, int) and g == 0):
                    pe.wait_ge(y_added, g)
                for t in range(TG):
                    mm = pe.matmul(y_ps[:, t * P:(t + 1) * P], hid[:, n, t * P:(t + 1) * P],
                                   down[:, c * P:(c + 1) * P], start=c == 0 and t == 0, stop=c == NC - 1,
                                   skip_group_check=True)
                mm.then_inc(down_done, 1)

            def body(g, q, more):
                for c in range(NC):
                    if more:
                        for s, f in (("turn", turn), ("logit", logit), ("lturn", lturn), ("cturn", cturn)):
                            if slot[s] == c:
                                f(g + 1, 1 - q)
                    if isinstance(g, int) and g < g0:
                        continue
                    up_and_gate(g, q, c)
                    if c > 0:
                        project(g, q, c - 1)
                    elif not (isinstance(g, int) and g == g0):
                        project(g - 1, 1 - q, NC - 1)
            body(g0 - 1, 1, True)
            body(g0, 0, True)
            body(g0 + 1, 1, True)
            with pe.Fori(1, NG // 2 - 1) as i:
                body(g0 + 2 * i, 0, True)
                body(g0 + 2 * i + 1, 1, True)
            body(g0 + NG - 2, 0, True)
            body(g0 + NG - 1, 1, False)
            project(g0 + NG - 1, 1, NC - 1)

        @block.scalar
        def _(act):
            def xh(g, q):
                act.wait_ge(xt_turned, g + 1)
                if not (isinstance(g, int) and g < 2):
                    act.wait_ge(up_done, (g - 1) * NC)
                act.activation(xh_sb[:, q, :], misc[:], ACT.Copy).then_inc(xh_done, 1)

            def lout(g, q):
                act.wait_ge(logits_t, g + 1)
                act.activation(logits[:], misc[:], ACT.Copy).then_inc(logits_out, 1)

            def r1(g, q):
                if first:
                    act.wait_ge(logits_turned, g + 1)
                    act.activation(th[:, :, 0:NE], misc3[:, :, 0:NE], ACT.Tanh, scale=0.5).then_inc(tanh_done, 1)

            def r2(g, q):
                if not first:
                    act.wait_ge(route, g * ROUTE + 4)
                    act.activation(th[:, :, 0:NE], df[:, :, 0:NE], ACT.Tanh).then_inc(tanh_done, 1)

            def cturn(g, q):
                act.wait_ge(comb_turned, g + 1)
                act.activation(combt[:, q, :], misc[:], ACT.Copy).then_inc(comb_t, 1)

            def silu(g, q, c):
                n = (q * NC + c) % 2
                num = g * NC + c
                act.wait_ge(gate_done, num + 1)
                if not (isinstance(num, int) and num < 2):
                    act.wait_ge(scaled, num - 1)
                act.activation(sil[:, n, :], gate_ps[:, n, :], ACT.Silu).then_inc(silu_done, 1)

            def body(g, q, more):
                for c in range(NC):
                    if not (isinstance(g, int) and g < g0):
                        silu(g, q, c)
                    if more:
                        for s, f in (("xh", xh), ("lout", lout), ("r1", r1), ("r2", r2), ("cturn", cturn)):
                            if slot[s] == c:
                                f(g + 1, 1 - q)
            body(g0 - 1, 1, True)
            body(g0, 0, True)
            body(g0 + 1, 1, True)
            with act.Fori(1, NG // 2 - 1) as i:
                body(g0 + 2 * i, 0, True)
                body(g0 + 2 * i + 1, 1, True)
            body(g0 + NG - 2, 0, True)
            body(g0 + NG - 1, 1, False)

        @block.gpsimd
        def _(pool):
            def invert(g):
                pool.wait_ge(eps_done, g + 1)
                pool.tensor_tensor(rstd[:], veps[:], k.neghalf[:, 0:TG], ALU.pow).then_inc(rstd_done, 1)
            invert(g0)
            with pool.Fori(1, NG) as i:
                invert(g0 + i)

        @block.vector
        def _(dve):
            def stats(g, q):
                for t in range(TG):
                    ins = dve.bn_stats(st[:, t, :], k.x[:, bass.ds(rows(g) + t * P, P)])
                ins.then_inc(stats_done, 1)

            def aggr(g, q):
                dve.wait_ge(stats_done, g + 1)
                pause(dve, k)
                for t in range(TG):
                    ins = dve.bn_aggr(mv[:, t, :], st[:, t, :])
                ins.then_inc(aggr_done, 1)
                dve.wait_ge(aggr_done, g + 1)
                dve.tensor_scalar(veps[:], mv[:, :, 1], EPS, None, ALU.add).then_inc(eps_done, 1)

            def norm(g, q):
                dve.wait_ge(rstd_done, g + 1)
                for t in range(TG):
                    ins = dve.tensor_scalar(xn[:, t, :], k.x[:, bass.ds(rows(g) + t * P, P)], mv[:, t, 0:1],
                                            rstd[:, t:t + 1], ALU.subtract, ALU.mult)
                ins.then_inc(norm_done, 1)

            def xl(g, q):
                dve.wait_ge(xh_done, g + 1)
                dve.tensor_tensor(xl_sb[:, q, :], misc[:], xh_sb[:, q, :].bitcast(F32), ALU.subtract)\
                   .then_inc(xl_done, 1)

            count = [0]

            def step(ins, g):
                count[0] += 1
                ins.then_inc(route, 1)
                dve.wait_ge(route, g * ROUTE + count[0])

            def top(g, width, dst):
                pause(dve, k)
                for t in range(TG):
                    ins = dve.max(dst[:, t, :], width[:, t, :])
                return ins

            def r1(g, q):
                count[0] = 0
                if first:
                    dve.wait_ge(tanh_done, g + 1)
                    step(dve.tensor_scalar(sig[:, :, 0:NE], th[:, :, 0:NE], 0.5, 0.5, ALU.mult, ALU.add), g)
                    step(dve.tensor_tensor(ext[:, :, 0:NE], sig[:, :, 0:NE],
                                           k.gate_bias[:].unsqueeze(1).broadcast_to([P, TG, NE]), ALU.add), g)
                    step(dve.tensor_reduce(gext[:, :, 0:4], ext[:, :, 0:NE].rearrange("p t (g e) -> p t g e", e=4),
                                           AX.X, ALU.max), g)
                else:
                    dve.wait_ge(logits_turned, g + 1)
                    step(dve.tensor_copy(ext[:, :, 0:NE], misc3[:, :, 0:NE]), g)
                    step(top(g, ext, top_sb), g)

            def r2(g, q):
                if first:
                    step(top(g, gext, top_sb), g)
                    step(dve.memset(top_sb[:, :, 2:8], PAD), g)
                    pause(dve, k)
                    for t in range(TG):
                        ins = dve.match_replace(gmark[:, t, :], top_sb[:, t, :], gext[:, t, :], TAKEN)
                    step(ins, g)
                    step(dve.tensor_scalar(pen[:], gmark[:, :, 0:4], TAKEN, OUT, ALU.not_equal, ALU.mult), g)
                else:
                    step(dve.tensor_tensor(hs[:], top_sb[:, :, 0:1], top_sb[:, :, 1:2], ALU.add), g)
                    step(dve.scalar_tensor_tensor(df[:], hs[:].broadcast_to([P, TG, E1]), -0.5,
                                                  ext[:, :, 0:NE], ALU.mult, ALU.add), g)

            def r3(g, q):
                if first:
                    step(dve.tensor_tensor(ext[:, :, 0:NE].rearrange("p t (g e) -> p t g e", e=4),
                                           ext[:, :, 0:NE].rearrange("p t (g e) -> p t g e", e=4),
                                           pen[:].unsqueeze(3).broadcast_to([P, TG, 4, 4]), ALU.add), g)
                    step(top(g, ext, top_sb), g)
                    step(dve.memset(top_sb[:, :, 4:8], PAD), g)
                else:
                    step(dve.memset(top_sb[:, :, 2:8], PAD), g)
                pause(dve, k)
                for t in range(TG):
                    ins = dve.match_replace(mark[:, t, :], top_sb[:, t, :], ext[:, t, :], TAKEN)
                step(ins, g)
                if not first:
                    dve.wait_ge(tanh_done, g + 1)
                    step(dve.tensor_scalar(sig[:, :, 0:NE], th[:, :, 0:NE], 0.5, 0.5, ALU.mult, ALU.add), g)

            def r4(g, q):
                ins = dve.scalar_tensor_tensor(comb[:, :, 0:NE], mark[:, :, 0:NE], TAKEN, sig[:, :, 0:NE],
                                               ALU.is_equal, ALU.mult)
                ins.then_inc(comb_done, 1)
                dve.wait_ge(comb_done, g + 1)
                if not (isinstance(g, int) and g == 0):
                    dve.wait_ge(comb_turned, g)
                dve.tensor_copy(cstack[:, :, 0:NE].bitcast(F32R), comb[:, :, 0:NE]).then_inc(comb_high, 1)
                dve.wait_ge(comb_high, g + 1)
                dve.tensor_tensor(cstack[:, :, 32:32 + NE].bitcast(F32R), comb[:, :, 0:NE],
                                  cstack[:, :, 0:NE], ALU.subtract).then_inc(route, 1)
                count[0] += 1
                assert count[0] == ROUTE, count[0]

            def add(g):
                dve.wait_ge(down_done, (g + 1) * NC)
                dve.scalar_tensor_tensor(k.x[:, bass.ds(rows(g), G)], y_ps[:], 0.5, k.x[:, bass.ds(rows(g), G)],
                                         ALU.mult, ALU.add).then_inc(y_added, 1)

            def scale(g, q, c):
                n = (q * NC + c) % 2
                num = g * NC + c
                dve.wait_ge(silu_done, num + 1)
                dve.wait_ge(up_done, num + 1)
                dve.tensor_tensor(scl[:, n, :], sil[:, n, :], comb_ps[:, n, :], ALU.mult).then_inc(scaled, 1)

            def hide(g, q, c):
                n = (q * NC + c) % 2
                num = g * NC + c
                dve.wait_ge(scaled, num + 1)
                if not (isinstance(num, int) and num < 2):
                    dve.wait_ge(down_done, num - 1)
                dve.tensor_tensor(hid[:, n, :], scl[:, n, :], up_ps[:, n, :], ALU.mult).then_inc(hidden, 1)

            def body(g, q, more):
                real = not (isinstance(g, int) and g < g0)
                for c in range(NC):
                    if real and slot["y"] == c and not (isinstance(g, int) and g == g0):
                        add(g - 1)
                    if real:
                        scale(g, q, c)
                    if more:
                        for s, f in (("stats", stats), ("aggr", aggr), ("norm", norm), ("xl", xl), ("r1", r1),
                                     ("r2", r2), ("r3", r3), ("r4", r4)):
                            if slot[s] == c:
                                f(g + 1, 1 - q)
                    if real:
                        hide(g, q, c)

            dve.memset(ext[:], PAD)
            dve.memset(gext[:], PAD)
            dve.memset(cstack[:], 0.0).then_inc(stack_cleared, 1)
            dve.wait_ge(stack_cleared, turn_no + 1)
            if first:
                dve.memset(cstack[:, :, E0:E0 + 1], 1.0)
            body(g0 - 1, 1, True)
            body(g0, 0, True)
            body(g0 + 1, 1, True)
            with dve.Fori(1, NG // 2 - 1) as i:
                body(g0 + 2 * i, 0, True)
                body(g0 + 2 * i + 1, 1, True)
            body(g0 + NG - 2, 0, True)
            body(g0 + NG - 1, 1, False)
            add(g0 + NG - 1)


def phase_attention(nc, k, a):
    NB = S // P
    HALF = S // G
    MAXU = [(t, c) for t in range(NB) for c in range(t // TG + 1)]
    UNITS = [(qg, kb) for qg in range(HALF) for kb in range(TG * (qg + 1))]
    NU = len(UNITS)
    SCALE = float(np.float32(1.0 / np.sqrt(DH)))

    PREP = [("proj", w, h) for w in range(2) for h in range(HALF)] + \
           [("max", j, u) for j in range(HG) for u in range(len(MAXU))] + [("maxt", 0, 0)]
    NEXT = [("ln", 0, h) for h in range(HALF)] + [("vt", 0, h) for h in range(HALF)]

    def section(hg):
        prep = list(PREP)
        out = [("vtok", 0, h) for h in range(HALF)] if hg == 0 else []
        for u in range(NU):
            out.append(("score", u, 0))
            if u > 0:
                out.append(("pv", u - 1, 0))
            elif hg > 0:
                out.append(("pv", NU - 1, -1))
            if u == 1 and hg > 0:
                out += [("oevac", 1, -1), ("ot", 1, -1)]
            if hg == 2 and u == 6:
                out.append(("stats", 0, 0))
            if hg == 2 and u == 9:
                out.append(("norm", 0, 0))
            if hg == 3 and u == 0:
                out += NEXT
            if u == (1 if hg == 3 else 0):
                out += prep[0:4]
            if 3 <= u <= 10:
                out += prep[4 + 6 * (u - 3):4 + 6 * (u - 2)]
            if u == 11:
                out.append(prep[-1])
            if u == 5:
                out += [("oevac", 0, 0), ("ot", 0, 0)]
        if hg == HG - 1:
            out += [("pv", NU - 1, 0), ("oevac", 1, 0), ("ot", 1, 0)]
            out += [("ont", 0, 0), ("ont", 0, 1), ("wo", 0, 0), ("wo", 0, 1)]
        return out

    SHARED = ("proj", "max", "maxt", "ln", "vt", "vtok", "ot", "ont", "wo")
    PROLOGUE = [("stats", 0, 0), ("norm", 0, 0)] + NEXT + PREP
    N0 = sum(e[0] in SHARED for e in PROLOGUE)
    BODY = [(hg, e) for hg in range(HG) for e in section(hg)]
    NBODY = sum(e[0] in SHARED for _, e in BODY)
    assert NBODY % 2 == 0

    with ExitStack() as ctx:
        def sb(name, shape, dt=F32):
            return ctx.enter_context(nc.sbuf_tensor(f"att_{name}", shape, dt))

        def sem(name):
            return ctx.enter_context(nc.semaphore(f"att_{name}"))

        w_raw, b_raw = sb("w_raw", [P, 4, D]), sb("b_raw", [1, 3 * D])
        wqk_h, wqk_l = sb("wqk_h", [P, 2, H * 32], F32R), sb("wqk_l", [P, 2, H * 32], F32R)
        wv_h, wv_l = sb("wv_h", [P, P], F32R), sb("wv_l", [P, P], F32R)
        wo_t = sb("wo_t", [P, P])
        bqk = sb("bqk", [P, 2, H * 32], F32R)
        ones = sb("ones", [P, G], F32R)
        bv, bo = sb("bv", [P, 1]), sb("bo", [P, D])
        ident_b, causal_b, causal_tb = sb("ident_b", [P, P], BF16), sb("causal_b", [P, P], BF16), \
            sb("causal_tb", [P, P], BF16)
        st, mv, veps, rstd = sb("st", [P, NB, 6]), sb("mv", [P, NB, 2]), sb("veps", [P, NB]), sb("rstd", [P, NB])
        xn = sb("xn", [P, NB, D])
        xn_h, xn_l = sb("xn_h", [P, S], F32R), sb("xn_l", [P, S], F32R)
        signed = sb("signed", [P, 2, G], F32R)
        q_st = sb("q_st", [P, 2, S], F32R)
        k_st = sb("k_st", [P, S], F32R)
        k_pad = sb("k_pad", [P, 2, HG, S], F32R)
        v_t, v_aug = sb("v_t", [P, S]), sb("v_aug", [P, NB, H, 32])
        mx, nm, mst = sb("mx", [P, HG, NB, 2]), sb("nm", [P, HG * NB]), sb("mst", [P, P])
        m_t = sb("m_t", [2 * HG * NB, P])
        probs = sb("probs", [P, 2, HG, G])
        o_sb, rec, o_tok = sb("o_sb", [P, 2, G]), sb("rec", [P, 2, TG, HG, 1]), sb("o_tok", [P, NB, D])
        on_t = sb("on_t", [P, S])
        y, ypos = sb("y", [P, TG, D]), sb("ypos", [P, TG, D])

        score_ps = k.banks[:, 0:4, :].rearrange("p (n h) c -> p n h c", n=2)
        shared, o_ps = k.banks[:, 4:6, :], k.banks[:, 6:8, :]

        w_in, turned, high_done, zeroed, ready = (sem(s) for s in ("w_in", "turned", "high_done", "zeroed", "ready"))
        with nc.Block() as block:
            @block.sync
            def _(sp):
                sp.dma_start(w_raw[:, 0:3, :], a["L0_attn_w_in"].rearrange("(w r) d -> r w d", r=P)).then_inc(w_in, 16)
                sp.dma_start(w_raw[:, 3, :], a["L0_attn_w_out"]).then_inc(w_in, 16)
                sp.dma_start(b_raw[:], a["L0_attn_b_in"].rearrange("(o n) -> o n", o=1)).then_inc(w_in, 16)
                sp.dma_start(bv[:], a["L0_attn_b_in"][2 * D:3 * D].rearrange("(n o) -> n o", o=1)).then_inc(w_in, 16)
                sp.dma_start(bo[:], a["L0_attn_b_out"].partition_broadcast(P)).then_inc(w_in, 16)

            @block.tensor
            def _(pe):
                pe.wait_ge(w_in, 80)
                for w in range(4):
                    mm = pe.transpose(shared[:, 0, w * P:(w + 1) * P], w_raw[:, w, :], k.ident)
                mm.then_inc(turned, 1)

            @block.gpsimd
            def _(pool):
                pool.memset(wqk_h[:].bitcast(F32), 0.0)
                pool.memset(wqk_l[:].bitcast(F32), 0.0)
                pool.memset(bqk[:].bitcast(F32), 0.0).then_inc(zeroed, 1)
                pool.memset(k_pad[:].bitcast(F32), 0.0)
                pool.memset(v_aug[:], 0.0).then_inc(zeroed, 1)
                pool.wait_ge(zeroed, 2)
                pool.memset(v_aug[:, :, :, DH:DH + 1], 1.0)
                pool.memset(mx[:], -3e38)
                pool.memset(mst[:], 0.0)

            @block.scalar
            def _(act):
                act.wait_ge(turned, 1)
                act.wait_ge(zeroed, 1)
                for w in range(2):
                    src = shared[:, 0, w * P:(w + 1) * P].rearrange("p (h d) -> p h d", d=DH)
                    row = b_raw[0:1, w * D:(w + 1) * D].rearrange("p (h d) -> p h d", d=DH)
                    for r in range(3):
                        cut = slice(r * DH, (r + 1) * DH)
                        act.activation(wqk_h[:, w, :].rearrange("p (h c) -> p h c", c=32)[:, :, cut], src, ACT.Copy)
                        act.activation(bqk[0:1, w, :].rearrange("p (h c) -> p h c", c=32)[:, :, cut], row, ACT.Copy)
                act.activation(wv_h[:], shared[:, 0, 2 * P:3 * P], ACT.Copy)
                act.activation(wo_t[:], shared[:, 0, 3 * P:4 * P], ACT.Copy).then_inc(high_done, 1)

            @block.vector
            def _(dve):
                dve.memset(ones[:].bitcast(F32), 1.0)
                dve.tensor_copy(ident_b[:], k.ident)
                dve.tensor_copy(causal_b[:], k.const("causal"))
                dve.tensor_copy(causal_tb[:], k.const("causalT"))
                dve.wait_ge(high_done, 1)
                for w in range(2):
                    src = shared[:, 0, w * P:(w + 1) * P].rearrange("p (h d) -> p h d", d=DH)
                    row = b_raw[0:1, w * D:(w + 1) * D].rearrange("p (h d) -> p h d", d=DH)
                    wh = wqk_h[:, w, :].rearrange("p (h c) -> p h c", c=32)
                    wl = wqk_l[:, w, :].rearrange("p (h c) -> p h c", c=32)
                    b3 = bqk[:, w, :].rearrange("p (h c) -> p h c", c=32)
                    for r in range(3):
                        cut = slice(r * DH, (r + 1) * DH)
                        dve.tensor_tensor(wl[:, :, cut], src, wh[:, :, cut].bitcast(F32), ALU.subtract)
                        dve.tensor_tensor(b3[32:33, :, cut], row, b3[0:1, :, cut].bitcast(F32), ALU.subtract)
                dve.memset(bqk[0:1, 1, :].rearrange("p (h c) -> p h c", c=32)[:, :, 24:26].bitcast(F32), 1.0)
                dve.tensor_tensor(wv_l[:], shared[:, 0, 2 * P:3 * P], wv_h[:].bitcast(F32), ALU.subtract)

        filled = [sem(f"filled{n}") for n in range(2)]
        emptied = [sem(f"emptied{n}") for n in range(2)]
        ln_steps, rstd_done = sem("ln_steps"), sem("rstd_done")
        signed_done, padded = sem("signed_done"), sem("padded")
        neg_steps, max_in = sem("neg_steps"), sem("max_in")
        scored, exped, attended = sem("scored"), sem("exped"), sem("attended")
        o_read, rec_done, y_steps = sem("o_read"), sem("rec_done"), sem("y_steps")
        xh_done, aggr_done = sem("xh_done"), sem("aggr_done")

        def walk(eng, parts):
            def run(entries, b, first):
                use = first
                for hg, (kind, x, z) in entries:
                    if kind in parts:
                        parts[kind](b, hg, x, z, use)
                    if kind in SHARED:
                        use += 1

            run([(-1, e) for e in PROLOGUE], 0, 0)
            with eng.Fori(0, B - 1) as b:
                run(BODY, b, N0)
            last = [e for e in BODY if e[0] < HG - 1 or (e[1] not in PREP and e[1] not in NEXT)]
            last = [(hg, e) for hg, e in last if not (e[0] in ("stats", "norm"))]
            run(last, B - 1, N0)

        def use_of(b, hg, use):
            return use % 2, use // 2 + (b * (NBODY // 2) if hg >= 0 else 0)

        def fill(pe, b, hg, use):
            q, before = use_of(b, hg, use)
            if not (isinstance(before, int) and before == 0):
                pe.wait_ge(emptied[q], before)
            return shared[:, q, :], filled[q]

        def content(eng, b, hg, use):
            q, before = use_of(b, hg, use)
            eng.wait_ge(filled[q], before + 1)
            return shared[:, q, :], emptied[q]

        def nxt(b, hg):
            return (0, 0) if hg < 0 else (b * HG + hg + 1, (hg + 1) % 2)

        block = ctx.enter_context(nc.Block())

        @block.tensor
        def _(pe):
            def ln(b, hg, _, h, use):
                bank, full = fill(pe, b, hg, use)
                n = 0 if hg < 0 else b + 1
                pe.wait_ge(ln_steps, 3 * n + 3)
                for t in range(TG):
                    mm = pe.transpose(bank[:, t * P:(t + 1) * P], xn[:, h * TG + t, :], k.ident)
                mm.then_inc(full, 1)

            def three(bank, full, wh, wl, h, more=None):
                mm = pe.matmul(bank, wh, xn_h[:, h * G:(h + 1) * G], start=True, stop=False)
                mm = pe.matmul(bank, wh, xn_l[:, h * G:(h + 1) * G], start=False, stop=False)
                mm = pe.matmul(bank, wl, xn_h[:, h * G:(h + 1) * G], start=False, stop=more is None)
                if more is not None:
                    mm = pe.matmul(bank, more, ones[:], start=False, stop=True)
                mm.then_inc(full, 1)

            def vt(b, hg, _, h, use):
                bank, full = fill(pe, b, hg, use)
                if h == 0:
                    q, before = use_of(b, hg, use - 1)
                    pe.wait_ge(emptied[q], before + 1)
                three(bank, full, wv_h[:], wv_l[:], h)

            def proj(b, hg, w, h, use):
                bank, full = fill(pe, b, hg, use)
                g = (hg + 1) % HG
                ws = slice(g * P, (g + 1) * P)
                three(bank, full, wqk_h[:, w, ws], wqk_l[:, w, ws], h, bqk[:, w, ws])

            def peak(b, hg, j, u, use):
                bank, full = fill(pe, b, hg, use)
                n, p = nxt(b, hg)
                if j == 0 and u == 0:
                    pe.wait_ge(padded, HG * n + HG)
                t, c = MAXU[u]
                width = min(G, (t + 1) * P - c * G)
                diag = c == t // TG
                mm = pe.matmul(bank[:, 0:width], q_st[:, p, t * P:(t + 1) * P], k_pad[:, p, j, c * G:c * G + width],
                               start=True, stop=not diag)
                if diag:
                    mm = pe.matmul(bank[:, width - P:width], ident_b[:], causal_b[:], start=False, stop=True)
                mm.then_inc(full, 1)

            def maxt(b, hg, _, __, use):
                bank, full = fill(pe, b, hg, use)
                n, p = nxt(b, hg)
                pe.wait_ge(neg_steps, 3 * n + 3)
                pe.transpose(bank[:, 0:P], mst[:], k.ident).then_inc(full, 1)

            def vtok(b, hg, _, h, use):
                bank, full = fill(pe, b, hg, use)
                for t in range(TG):
                    mm = pe.transpose(bank[:, t * P:(t + 1) * P], v_t[:, (h * TG + t) * P:(h * TG + t + 1) * P], k.ident)
                mm.then_inc(full, 1)

            def score(b, hg, u, _, use):
                p = hg % 2
                qg, kb = UNITS[u]
                r = max(0, kb - TG * qg)
                n = G - r * P
                if u == 0:
                    pe.wait_ge(max_in, 2 * HG * 16 * (b * HG + hg + 1))
                for pair in range(2):
                    pe.wait_ge(exped, ((b * HG + hg) * NU + u) * 2 + pair + 1)
                    for i in range(2):
                        j = pair * 2 + i
                        mm = pe.matmul(score_ps[:, pair, i, 0:n], k_pad[:, p, j, kb * P:(kb + 1) * P],
                                       q_st[:, p, qg * G + r * P:(qg + 1) * G], start=True, stop=kb < TG * qg)
                        if kb >= TG * qg:
                            mm = pe.matmul(score_ps[:, pair, i, 0:P], ident_b[:], causal_tb[:],
                                           start=False, stop=True)
                    mm.then_inc(scored, 1)

            def pv(b, hg, u, back, use):
                g = hg + back
                num = (b * HG + g) * NU + u
                qg, kb = UNITS[u]
                r = max(0, kb - TG * qg)
                pe.wait_ge(exped, 2 * num + 2 + 2)
                if kb == 0:
                    pe.wait_ge(o_read, 2 * (b * HG + g) + qg + 1)
                    if u == 0 and g == 0:
                        q, before = use_of(b, hg, HALF - 1 + N0)
                        pe.wait_ge(emptied[q], before + 1)
                for j in range(HG):
                    mm = pe.matmul(o_ps[32 * j:32 * j + 32, qg, r * P:G], v_aug[:, kb, g * HG + j, :],
                                   probs[:, u % 2, j, 0:G - r * P], start=kb == 0, stop=kb == TG * (qg + 1) - 1,
                                   tile_position=(0, 32 * j), skip_group_check=True)
                mm.then_inc(attended, 1)

            def ot(b, hg, qg, back, use):
                bank, full = fill(pe, b, hg, use)
                pe.wait_ge(o_read, 2 * (b * HG + hg + back) + qg + 3)
                for t in range(TG):
                    mm = pe.transpose(bank[:, t * P:(t + 1) * P], o_sb[:, qg, t * P:(t + 1) * P], k.ident)
                mm.then_inc(full, 1)

            def ont(b, hg, _, h, use):
                bank, full = fill(pe, b, hg, use)
                if h == 0:
                    q, before = use_of(b, hg, use - 1)
                    pe.wait_ge(emptied[q], before + 1)
                for t in range(TG):
                    mm = pe.transpose(bank[:, t * P:(t + 1) * P], o_tok[:, h * TG + t, :], k.ident)
                mm.then_inc(full, 1)

            def wo(b, hg, _, h, use):
                bank, full = fill(pe, b, hg, use)
                for t in range(TG):
                    mm = pe.matmul(bank[:, t * P:(t + 1) * P], on_t[:, (h * TG + t) * P:(h * TG + t + 1) * P], wo_t[:],
                                   start=True, stop=True, skip_group_check=True)
                mm.then_inc(full, 1)

            walk(pe, dict(ln=ln, vt=vt, proj=proj, max=peak, maxt=maxt, vtok=vtok, score=score, pv=pv, ot=ot,
                          ont=ont, wo=wo))

        @block.scalar
        def _(act):
            def ln(b, hg, _, h, use):
                q, before = use_of(b, hg, use)
                act.wait_ge(filled[q], before + 1)
                act.activation(xn_h[:, h * G:(h + 1) * G], shared[:, q, :], ACT.Copy).then_inc(xh_done, 1)

            def vt(b, hg, _, h, use):
                bank, empty = content(act, b, hg, use)
                act.activation(v_t[:, h * G:(h + 1) * G], bank, ACT.Identity, bias=bv[:, 0:1]).then_inc(empty, 1)

            def proj(b, hg, w, h, use):
                q, before = use_of(b, hg, use)
                act.wait_ge(filled[q], before + 1)
                act.activation(signed[:, h % 2, :], shared[:, q, :], ACT.Identity,
                               scale=k.const(("qsign", "ksign")[w])).then_inc(signed_done, 1)

            def maxt(b, hg, _, __, use):
                n, p = nxt(b, hg)
                if not (isinstance(n, int) and n == 0):
                    act.wait_ge(max_in, 2 * HG * 16 * n)
                bank, empty = content(act, b, hg, use)
                act.activation(m_t[:], bank[0:2 * HG * NB, 0:P], ACT.Copy).then_inc(empty, 1)

            def score(b, hg, u, _, use):
                num = (b * HG + hg) * NU + u
                qg, kb = UNITS[u]
                n = G - max(0, kb - TG * qg) * P
                act.wait_ge(attended, num + 1)
                for pair in range(2):
                    act.wait_ge(scored, 2 * num + pair + 1)
                    act.activation(probs[:, u % 2, 2 * pair:2 * pair + 2, 0:n], score_ps[:, pair, :, 0:n], ACT.Exp,
                                   scale=SCALE).then_inc(exped, 1)

            def oevac(b, hg, qg, back, use):
                g = b * HG + hg + back
                last = UNITS.index((qg, TG * (qg + 1) - 1))
                act.wait_ge(attended, g * NU + last + 1 + 2)
                act.activation(o_sb[:, qg, :], o_ps[:, qg, :], ACT.Copy).then_inc(o_read, 1)

            def ont(b, hg, _, h, use):
                bank, empty = content(act, b, hg, use)
                act.activation(on_t[:, h * G:(h + 1) * G], bank, ACT.Copy).then_inc(empty, 1)

            act.activation(y[:, 0, 0:1], k.ident[:, 0:1], ACT.Copy).then_inc(exped, 2)
            act.activation(y[:, 0, 1:2], k.ident[:, 0:1], ACT.Copy).then_inc(attended, 2)
            act.activation(y[:, 0, 2:3], k.ident[:, 0:1], ACT.Copy).then_inc(o_read, 2)
            walk(act, dict(ln=ln, vt=vt, proj=proj, maxt=maxt, score=score, oevac=oevac, ont=ont))

        @block.gpsimd
        def _(pool):
            def norm(b, hg, _, __, use):
                n = 0 if hg < 0 else b + 1
                pool.wait_ge(ln_steps, 3 * n + 2)
                pool.tensor_tensor(rstd[:], veps[:], k.neghalf[:, 0:NB], ALU.pow).then_inc(rstd_done, 1)

            def proj(b, hg, w, h, use):
                if w == 0 or h == 0:
                    return
                n, p = nxt(b, hg)
                for half in (use - 1, use):
                    q, before = use_of(b, hg, half)
                    pool.wait_ge(emptied[q], before + 1)
                pool.tensor_tensor(k.unread_pool[:], k.neghalf[0:32, 0:1], k.neghalf[0:32, 0:1], ALU.add)
                for j in range(HG):
                    rows = slice(32 * j, 32 * j + 32)
                    pool.tensor_copy(k_pad[rows, p, j, :], k_st[rows, :].bitcast(F32)).then_inc(padded, 1)

            walk(pool, dict(norm=norm, proj=proj))

        @block.sync
        def _(sp):
            def maxt(b, hg, _, __, use):
                n, p = nxt(b, hg)
                content(sp, b, hg, use)
                q, before = use_of(b, hg, use)
                sp.wait_ge(emptied[q], before + 1)
                for part in range(2):
                    for j in range(HG):
                        r = (part * HG + j) * NB
                        sp.dma_start(q_st[32 * j + 24 + part:32 * j + 25 + part, p, :].bitcast(F32),
                                     m_t[r:r + NB, :]).then_inc(max_in, 16)

            walk(sp, dict(maxt=maxt))

        @block.vector
        def _(dve):
            def stats(b, hg, _, __, use):
                n = 0 if hg < 0 else b + 1
                for t in range(NB):
                    ins = dve.bn_stats(st[:, t, :], k.x[:, bass.ds(n * S + t * P, P)])
                ins.then_inc(ln_steps, 1)
                dve.wait_ge(ln_steps, 3 * n + 1)
                pause(dve, k)
                for t in range(NB):
                    ins = dve.bn_aggr(mv[:, t, :], st[:, t, :])
                ins.then_inc(aggr_done, 1)
                dve.wait_ge(aggr_done, n + 1)
                dve.tensor_scalar(veps[:], mv[:, :, 1], EPS, None, ALU.add).then_inc(ln_steps, 1)

            def norm(b, hg, _, __, use):
                n = 0 if hg < 0 else b + 1
                dve.wait_ge(rstd_done, n + 1)
                for t in range(NB):
                    ins = dve.tensor_scalar(xn[:, t, :], k.x[:, bass.ds(n * S + t * P, P)], mv[:, t, 0:1],
                                            rstd[:, t:t + 1], ALU.subtract, ALU.mult)
                ins.then_inc(ln_steps, 1)

            def ln(b, hg, _, h, use):
                bank, empty = content(dve, b, hg, use)
                n = 0 if hg < 0 else b + 1
                dve.wait_ge(xh_done, 2 * n + h + 1)
                dve.tensor_tensor(xn_l[:, h * G:(h + 1) * G], bank, xn_h[:, h * G:(h + 1) * G].bitcast(F32),
                                  ALU.subtract).then_inc(empty, 1)

            def proj(b, hg, w, h, use):
                n, p = nxt(b, hg)
                bank, empty = content(dve, b, hg, use)
                dve.wait_ge(signed_done, 4 * n + w * HALF + h + 1)
                dst = (q_st[:, p, :], k_st[:])[w][:, h * G:(h + 1) * G]
                if w == 1 and h == 0 and hg >= 0:
                    dve.wait_ge(padded, HG * n)
                dve.scalar_tensor_tensor(dst, bank, k.const(("qlow", "klow")[w]), signed[:, h % 2, :].bitcast(F32),
                                         ALU.mult, ALU.add).then_inc(empty, 1)

            def peak(b, hg, j, u, use):
                bank, empty = content(dve, b, hg, use)
                t, c = MAXU[u]
                width = min(G, (t + 1) * P - c * G)
                dve.tensor_reduce(mx[:, j, t, c:c + 1], bank[:, 0:width], AX.X, ALU.max).then_inc(empty, 1)

            def maxt(b, hg, _, __, use):
                n, p = nxt(b, hg)
                for last in (use - 2, use - 1):
                    q, before = use_of(b, hg, last)
                    dve.wait_ge(emptied[q], before + 1)
                dve.tensor_reduce(nm[:], mx[:].rearrange("p j t c -> p (j t) c"), AX.X, ALU.max, negate=True)\
                   .then_inc(neg_steps, 1)
                dve.wait_ge(neg_steps, 3 * n + 1)
                dve.tensor_copy(mst[:, 0:HG * NB].bitcast(F32R), nm[:]).then_inc(neg_steps, 1)
                dve.wait_ge(neg_steps, 3 * n + 2)
                dve.tensor_tensor(mst[:, HG * NB:2 * HG * NB].bitcast(F32R), nm[:], mst[:, 0:HG * NB], ALU.subtract)\
                   .then_inc(neg_steps, 1)

            def vtok(b, hg, _, h, use):
                bank, empty = content(dve, b, hg, use)
                dve.tensor_copy(v_aug[:, h * TG:(h + 1) * TG, :, 0:DH],
                                bank.rearrange("p (t h d) -> p t h d", h=H, d=DH)).then_inc(empty, 1)

            def ot(b, hg, qg, back, use):
                bank, empty = content(dve, b, hg, use)
                g = hg + back
                o = bank.rearrange("p (t j d) -> p t j d", j=HG, d=32)
                dve.reciprocal(rec[:, qg], o[:, :, :, DH:DH + 1]).then_inc(rec_done, 1)
                dve.wait_ge(rec_done, 2 * (b * HG + g) + qg + 1)
                for t in range(TG):
                    ins = dve.tensor_tensor(o_tok[:, qg * TG + t, g * 32:g * 32 + 32].rearrange("p (j d) -> p j d", d=DH),
                                            o[:, t, :, 0:DH], rec[:, qg, t, :, :].broadcast_to([P, HG, DH]), ALU.mult)
                ins.then_inc(empty, 1)

            def wo(b, hg, _, h, use):
                bank, empty = content(dve, b, hg, use)
                xs = k.x[:, bass.ds(b * S + h * G, G)]
                base = (b * HALF + h) * 4
                dve.tensor_tensor(y[:], bank.rearrange("p (t d) -> p t d", d=D),
                                  bo[:].unsqueeze(1).broadcast_to([P, TG, D]), ALU.add).then_inc(empty, 1)
                q, before = use_of(b, hg, use)
                dve.wait_ge(emptied[q], before + 1)
                dve.tensor_scalar(ypos[:], y[:], 0.0, None, ALU.max).then_inc(y_steps, 1)
                dve.wait_ge(y_steps, base + 1)
                dve.scalar_tensor_tensor(ypos[:], y[:], 0.0, ypos[:], ALU.min, ALU.add).then_inc(y_steps, 1)
                dve.wait_ge(y_steps, base + 2)
                dve.tensor_tensor(xs, xs, ypos[:].rearrange("p t d -> p (t d)"), ALU.add).then_inc(y_steps, 2)
                dve.wait_ge(y_steps, base + 4)

            walk(dve, dict(stats=stats, norm=norm, ln=ln, proj=proj, max=peak, maxt=maxt, vtok=vtok, ot=ot, wo=wo))


def phase_gated(nc, k, a):
    NB = S // P
    HALF = S // G
    EC = HV // P
    NBANK = 7
    BLOCKS = ((0, 0, 0), (0, 32, 1), (1, 0, 2), (1, 64, 3))

    BODY = [("norm", r, 0) for r in range(2)] + [("ln", 0, h) for h in range(HALF)]
    BODY += [("proj", v, h) for h in range(HALF) for v in range(4)]
    BODY += [("v", 0, t) for t in range(NB // 2)]
    BODY += [("gate", c, h) for c in range(EC) for h in range(HALF)]
    BODY += [("ktok", 0, h) for h in range(HALF)] + [("att", 0, h) for h in range(HALF)] + [("kv", 0, 0)]
    BODY += [("out", c, h) for h in range(HALF) for c in range(EC)] + [("y", 0, h) for h in range(HALF)]
    SHARED = ("ln", "proj", "v", "gate", "ktok", "att", "out", "y")
    NBODY = sum(e[0] in SHARED for e in BODY)
    assert NBODY % NBANK == 0

    with ExitStack() as ctx:
        def sb(name, shape, dt=F32):
            return ctx.enter_context(nc.sbuf_tensor(f"gau_{name}", shape, dt))

        def sem(name):
            return ctx.enter_context(nc.semaphore(f"gau_{name}"))

        lay, _ = pack_layout()
        wqk_raw, wv_raw, wg_raw, wo_raw = (sb("wqk_raw", [P, P]), sb("wv_raw", [P, EC, P]), sb("wg_raw", [P, EC, P]),
                                           sb("wo_raw", [P, HV]))
        wqk_h, wqk_l = sb("wqk_h", [P, 4, P], F32R), sb("wqk_l", [P, 4, P], F32R)
        wv_h, wv_l = sb("wv_h", [P, HV], F32R), sb("wv_l", [P, HV], F32R)
        wg_h, wg_l = sb("wg_h", [P, HV], F32R), sb("wg_l", [P, HV], F32R)
        wo_t = sb("wo_t", [P, HV])
        par = sb("par", [P, 4, 3])
        ln1w, ln1b, bg = sb("ln1w", [P, 1]), sb("ln1b", [P, 1]), sb("bg", [P, EC])
        bv_raw, bv_row, ones = sb("bv_raw", [1, HV]), sb("bv_row", [P, HV], F32R), sb("ones", [P, P], F32R)
        bo, ln2w, ln2b = sb("bo", [P, D]), sb("ln2w", [P, D]), sb("ln2b", [P, D])
        pos, dval = sb("pos", [P, NPOS]), sb("dval", [P, NPOS])
        rel, picked = sb("rel", [P, P]), sb("picked", [P, P])
        cos, sin = sb("cos", [P, S]), sb("sin", [P, S])
        st, mv, veps, rstd = sb("st", [P, NB, 6]), sb("mv", [P, NB, 2]), sb("veps", [P, NB]), sb("rstd", [P, NB])
        xn, xn2 = sb("xn", [P, NB, D]), sb("xn2", [P, NB, D])
        xt = sb("xt", [P, 2, G])
        x_h, x_l = sb("x_h", [P, S], F32R), sb("x_l", [P, S], F32R)
        act_s, head, turned_s = sb("act_s", [P, 2, G]), sb("head", [P, 2, G]), sb("turned_s", [P, 2, G])
        stack = sb("stack", [P, 2, S])
        v_tok, gate = sb("v_tok", [P, NB, HV]), sb("gate", [P, EC, S])
        k_tok, kv = sb("k_tok", [P, NB, P]), sb("kv", [P, HV])
        att_s, att = sb("att_s", [P, 2, G]), sb("att", [P, 2, G])
        mixed = sb("mixed", [P, 2, EC, G])
        y, yn = sb("y", [P, 2, TG, D]), sb("yn", [P, 2, TG, D])
        st2, mv2, veps2, rstd2 = (sb("st2", [P, 2, TG, 6]), sb("mv2", [P, 2, TG, 2]), sb("veps2", [P, 2, TG]),
                                  sb("rstd2", [P, 2, TG]))
        flag = sb("flag", [P, 16])
        shared, kv_ps = k.banks[:, 0:NBANK, :], k.banks[:, NBANK, 0:HV]

        w_in, p_in, zeroed, turned, high_done, rel_steps = (sem(s) for s in
            ("w_in", "p_in", "zeroed", "turned", "high_done", "rel_steps"))
        params = ("L1_attn_bqk", "L1_attn_gamma", "L1_attn_beta")
        half = QK // 2
        with nc.Block() as block:
            @block.sync
            def _(sp):
                sp.wait_ge(zeroed, 1)
                sp.dma_start(wqk_raw[0:QK, :], a["L1_attn_Wqk"]).then_inc(w_in, 16)
                sp.dma_start(wv_raw[:], a["L1_attn_Wv"].rearrange("(c p) d -> p c d", p=P)).then_inc(w_in, 16)
                sp.dma_start(wg_raw[:], a["L1_attn_Wg"].rearrange("(c p) d -> p c d", p=P)).then_inc(w_in, 16)
                sp.dma_start(wo_raw[:], a["L1_attn_Wo"]).then_inc(w_in, 16)
                sp.dma_start(bv_raw[:], a["L1_attn_bv"].rearrange("(o n) -> o n", o=1)).then_inc(w_in, 16)
                for c in range(EC):
                    sp.dma_start(bg[:, c:c + 1], a["L1_attn_bg"][c * P:(c + 1) * P].rearrange("(n o) -> n o", o=1))\
                      .then_inc(w_in, 16)
                sp.dma_start(ln1w[:], a["L1_attn_ln1_w"].rearrange("(n o) -> n o", o=1)).then_inc(w_in, 16)
                sp.dma_start(ln1b[:], a["L1_attn_ln1_b"].rearrange("(n o) -> n o", o=1)).then_inc(w_in, 16)
                sp.dma_start(bo[:], a["L1_attn_bo"].partition_broadcast(P)).then_inc(w_in, 16)
                sp.dma_start(ln2w[:], a["L1_attn_ln2_w"].partition_broadcast(P)).then_inc(w_in, 16)
                sp.dma_start(ln2b[:], a["L1_attn_ln2_b"].partition_broadcast(P)).then_inc(w_in, 16)
                sp.dma_start(pos[:], a["L1_attn_pos_emb"][0:NPOS].partition_broadcast(P)).then_inc(w_in, 16)
                sp.dma_start(cos[:], a["consts"][:, slice(*lay["cos"])]).then_inc(w_in, 16)
                sp.dma_start(sin[:], a["consts"][:, slice(*lay["sin"])]).then_inc(w_in, 16)
                sp.dma_start(dval[:], a["consts"][:, slice(*lay["dval"])]).then_inc(w_in, 16)

            @block.scalar
            def _(act):
                act.wait_ge(zeroed, 1)
                n = 0
                for stk, row, which in BLOCKS:
                    for swap in range(2):
                        for c, name in enumerate(params):
                            src = a[name] if c == 0 else a[name][which]
                            for part in range(2):
                                to = row + half * (part ^ swap)
                                act.dma_start(par[to:to + half, 2 * stk + swap, c:c + 1],
                                              src[part * half:(part + 1) * half].rearrange("(n o) -> n o", o=1))\
                                   .then_inc(p_in, 16)
                                n += 1
                act.wait_ge(turned, 1)
                src = shared[:, 0, 0:QK].rearrange("p (s n) -> p s n", n=half)
                for stk, row, which in BLOCKS:
                    act.activation(wqk_h[:, 2 * stk, row:row + QK], shared[:, 0, 0:QK], ACT.Copy)
                    for part in range(2):
                        to = row + half * (1 - part)
                        act.activation(wqk_h[:, 2 * stk + 1, to:to + half], src[:, part, :], ACT.Copy)
                act.activation(wv_h[:], shared[:, 1, 0:HV], ACT.Copy)
                act.activation(wg_h[:], shared[:, 1, HV:2 * HV], ACT.Copy)
                act.activation(bv_row[0:1, :], bv_raw[:], ACT.Copy)
                act.activation(wo_t[:], shared[:, 2, 0:HV], ACT.Copy).then_inc(high_done, 1)
                act.wait_ge(p_in, 16 * n)

            @block.gpsimd
            def _(pool):
                pool.memset(wqk_raw[:], 0.0)
                pool.memset(par[:], 0.0)
                pool.memset(wqk_h[:].bitcast(F32), 0.0)
                pool.memset(wqk_l[:].bitcast(F32), 0.0)
                pool.memset(bv_row[:].bitcast(F32), 0.0).then_inc(zeroed, 1)
                pool.memset(ones[:].bitcast(F32), 1.0)
                pool.memset(kv[:], 0.0)

            @block.tensor
            def _(pe):
                pe.wait_ge(w_in, 16 * 16)
                pe.transpose(shared[:, 0, 0:P], wqk_raw[:], k.ident)
                for c in range(EC):
                    pe.transpose(shared[:, 1, c * P:(c + 1) * P], wv_raw[:, c, :], k.ident)
                    pe.transpose(shared[:, 1, HV + c * P:HV + (c + 1) * P], wg_raw[:, c, :], k.ident)
                    mm = pe.transpose(shared[:, 2, c * P:(c + 1) * P], wo_raw[:, c * P:(c + 1) * P], k.ident)
                mm.then_inc(turned, 1)

            @block.vector
            def _(dve):
                dve.wait_ge(high_done, 1)
                src = shared[:, 0, 0:QK].rearrange("p (s n) -> p s n", n=half)
                for stk, row, which in BLOCKS:
                    dve.tensor_tensor(wqk_l[:, 2 * stk, row:row + QK], shared[:, 0, 0:QK],
                                      wqk_h[:, 2 * stk, row:row + QK].bitcast(F32), ALU.subtract)
                    for part in range(2):
                        to = row + half * (1 - part)
                        dve.tensor_tensor(wqk_l[:, 2 * stk + 1, to:to + half], src[:, part, :],
                                          wqk_h[:, 2 * stk + 1, to:to + half].bitcast(F32), ALU.subtract)
                dve.tensor_tensor(wv_l[:], shared[:, 1, 0:HV], wv_h[:].bitcast(F32), ALU.subtract)
                dve.tensor_tensor(wg_l[:], shared[:, 1, HV:2 * HV], wg_h[:].bitcast(F32), ALU.subtract)
                dve.tensor_tensor(bv_row[32:33, :], bv_raw[:], bv_row[0:1, :].bitcast(F32), ALU.subtract)
                dve.wait_ge(w_in, 16 * 16)
                dve.tensor_copy(rel[:], k.const("outside")).then_inc(rel_steps, 2)
                dve.wait_ge(rel_steps, 2)
                with dve.Fori(0, NPOS) as i:
                    dve.tensor_scalar(picked[:], k.const("dist"), dval[:, bass.ds(i, 1)], pos[:, bass.ds(i, 1)],
                                      ALU.is_equal, ALU.mult).then_inc(rel_steps, 1)
                    dve.wait_ge(rel_steps, 2 * i + 3)
                    dve.tensor_tensor(rel[:], rel[:], picked[:], ALU.add).then_inc(rel_steps, 1)
                    dve.wait_ge(rel_steps, 2 * i + 4)

        filled = [sem(f"filled{n}") for n in range(NBANK)]
        emptied = [sem(f"emptied{n}") for n in range(NBANK)]
        ln_steps, rstd_done, xt_done, x_h_done, x_l_done = (sem(s) for s in
            ("ln_steps", "rstd_done", "xt_done", "x_h_done", "x_l_done"))
        silu_done, rot = sem("silu_done"), sem("rot")
        kv_done, kv_out, att_steps = sem("kv_done"), sem("kv_out"), sem("att_steps")
        y_steps, rstd2_done = sem("y_steps"), sem("rstd2_done")
        LN = 4
        ROT = 5
        YS = 8

        def walk(eng, parts):
            with eng.Fori(0, B) as b:
                use = 0
                for kind, x, z in BODY:
                    if kind in parts:
                        parts[kind](b, x, z, use)
                    if kind in SHARED:
                        use += 1

        def use_of(b, use):
            return use % NBANK, use // NBANK + b * (NBODY // NBANK)

        def fill(pe, b, use):
            q, before = use_of(b, use)
            pe.wait_ge(emptied[q], before + 1)
            return shared[:, q, :], filled[q]

        def content(eng, b, use):
            q, before = use_of(b, use)
            eng.wait_ge(filled[q], before + 1)
            return shared[:, q, :], emptied[q]

        def was_read(eng, b, use):
            q, before = use_of(b, use)
            eng.wait_ge(emptied[q], before + 2)

        block = ctx.enter_context(nc.Block())

        @block.tensor
        def _(pe):
            def ln(b, _, h, use):
                bank, full = fill(pe, b, use)
                pe.wait_ge(ln_steps, 2 * LN * (b + 1))
                for t in range(TG):
                    mm = pe.transpose(bank[:, t * P:(t + 1) * P], xn2[:, h * TG + t, :], k.ident)
                mm.then_inc(full, 1)

            def three(bank, full, wh, wl, h):
                pe.matmul(bank, wh, x_h[:, h * G:(h + 1) * G], start=True, stop=False)
                pe.matmul(bank, wh, x_l[:, h * G:(h + 1) * G], start=False, stop=False)
                pe.matmul(bank, wl, x_h[:, h * G:(h + 1) * G], start=False, stop=True).then_inc(full, 1)

            def proj(b, v, h, use):
                bank, full = fill(pe, b, use)
                pe.wait_ge(x_l_done, HALF * b + h + 1)
                three(bank, full, wqk_h[:, v, :], wqk_l[:, v, :], h)

            def val(b, _, t2, use):
                bank, full = fill(pe, b, use)
                for i in range(2):
                    tok = slice((2 * t2 + i) * P, (2 * t2 + i + 1) * P)
                    to = bank[:, i * HV:(i + 1) * HV]
                    pe.matmul(to, x_h[:, tok], wv_h[:], start=True, stop=False)
                    pe.matmul(to, x_l[:, tok], wv_h[:], start=False, stop=False)
                    pe.matmul(to, x_h[:, tok], wv_l[:], start=False, stop=False)
                    mm = pe.matmul(to, ones[:], bv_row[:], start=False, stop=True)
                mm.then_inc(full, 1)

            def gates(b, c, h, use):
                bank, full = fill(pe, b, use)
                three(bank, full, wg_h[:, c * P:(c + 1) * P], wg_l[:, c * P:(c + 1) * P], h)

            def ktok(b, _, h, use):
                bank, full = fill(pe, b, use)
                pe.wait_ge(rot, (HALF * 2 * b + 2 * h + 2) * ROT + ROT)
                for t in range(TG):
                    mm = pe.transpose(bank[:, t * P:(t + 1) * P], stack[:, 1, (h * TG + t) * P:(h * TG + t + 1) * P],
                                      k.ident)
                mm.then_inc(full, 1)

            def attn(b, _, h, use):
                bank, full = fill(pe, b, use)
                for t in range(TG):
                    tok = slice((h * TG + t) * P, (h * TG + t + 1) * P)
                    mm = pe.matmul(bank[:, t * P:(t + 1) * P], stack[:, 1, tok], stack[:, 0, tok], start=True,
                                   stop=True, skip_group_check=True)
                mm.then_inc(full, 1)

            def kvs(b, _, __, use):
                was_read(pe, b, use - 3)
                was_read(pe, b, use - 4)
                pe.wait_ge(kv_out, b + 1)
                for t in range(NB):
                    mm = pe.matmul(kv_ps[:], k_tok[:, t, :], v_tok[:, t, :], start=t == 0, stop=t == NB - 1)
                mm.then_inc(kv_done, 1)

            def out(b, c, h, use):
                bank, full = fill(pe, b, use)
                if h == 0 and c == 0:
                    pe.wait_ge(kv_out, b + 2)
                pe.wait_ge(att_steps, 2 * (HALF * b + h + 1))
                pe.matmul(bank, kv[:, c * P:(c + 1) * P], stack[:, 0, h * G:(h + 1) * G], start=True, stop=False,
                          skip_group_check=True)
                for t in range(TG):
                    mm = pe.matmul(bank[:, t * P:(t + 1) * P], v_tok[:, h * TG + t, c * P:(c + 1) * P],
                                   att[:, h, t * P:(t + 1) * P], start=False, stop=True, skip_group_check=True)
                mm.then_inc(full, 1)

            def ys(b, _, h, use):
                bank, full = fill(pe, b, use)
                for c in range(EC):
                    was_read(pe, b, use - HALF * EC + h * (EC - 1) + c)
                for t in range(TG):
                    for c in range(EC):
                        mm = pe.matmul(bank[:, t * P:(t + 1) * P], mixed[:, h, c, t * P:(t + 1) * P],
                                       wo_t[:, c * P:(c + 1) * P], start=t == 0 and c == 0, stop=c == EC - 1,
                                       skip_group_check=True)
                mm.then_inc(full, 1)

            walk(pe, dict(ln=ln, proj=proj, v=val, gate=gates, ktok=ktok, att=attn, kv=kvs, out=out, y=ys))

        @block.scalar
        def _(act):
            def ln(b, _, h, use):
                bank, empty = content(act, b, use)
                act.activation(xt[:, h, :], bank, ACT.Identity, bias=ln1b[:, 0:1], scale=ln1w[:, 0:1])\
                   .then_inc(empty, 1)
                was_read(act, b, use)
                act.activation(x_h[:, h * G:(h + 1) * G], xt[:, h, :], ACT.Copy).then_inc(x_h_done, 1)

            def proj(b, v, h, use):
                bank, empty = content(act, b, use)
                act.wait_ge(rot, (HALF * 2 * b + 2 * h + v // 2) * ROT + 1 + v % 2)
                act.activation(act_s[:, v % 2, :], bank, ACT.Silu, bias=par[:, v, 0:1]).then_inc(empty, 1)

            def val(b, _, t2, use):
                bank, empty = content(act, b, use)
                act.activation(v_tok[:, 2 * t2:2 * t2 + 2, :], bank.rearrange("p (t e) -> p t e", t=2), ACT.Silu)\
                   .then_inc(empty, 1)

            def gates(b, c, h, use):
                bank, empty = content(act, b, use)
                act.activation(gate[:, c, h * G:(h + 1) * G], bank, ACT.Silu, bias=bg[:, c:c + 1]).then_inc(empty, 1)

            def ktok(b, _, h, use):
                bank, empty = content(act, b, use)
                act.activation(k_tok[:, h * TG:(h + 1) * TG, :], bank.rearrange("p (t r) -> p t r", t=TG), ACT.Copy)\
                   .then_inc(empty, 1)

            def kvs(b, _, __, use):
                act.wait_ge(kv_done, b + 1)
                act.activation(kv[32:64, :], kv_ps[64:96, :], ACT.Copy, scale=1.0 / S).then_inc(kv_out, 1)

            act.activation(kv[0:1, 0:1], k.const("qlow")[0:1, :], ACT.Copy).then_inc(kv_out, 1)
            walk(act, dict(ln=ln, proj=proj, v=val, gate=gates, ktok=ktok, kv=kvs))

        @block.gpsimd
        def _(pool):
            def norm(b, r, _, use):
                n = 2 * b + r
                pool.wait_ge(ln_steps, n * LN + 3)
                pool.tensor_tensor(rstd[:], veps[:], k.neghalf[:, 0:NB], ALU.pow).then_inc(rstd_done, 1)

            def ys(b, _, h, use):
                n = HALF * b + h
                pool.wait_ge(y_steps, n * YS + 4)
                pool.tensor_tensor(rstd2[:, h, :], veps2[:, h, :], k.neghalf[:, 0:TG], ALU.pow).then_inc(rstd2_done, 1)

            walk(pool, dict(norm=norm, y=ys))

        @block.vector
        def _(dve):
            def norm(b, r, _, use):
                n = 2 * b + r

                def src(t):
                    return k.x[:, bass.ds(b * S + t * P, P)] if r == 0 else xn[:, t, :]

                for t in range(NB):
                    ins = dve.bn_stats(st[:, t, :], src(t))
                ins.then_inc(ln_steps, 1)
                dve.wait_ge(ln_steps, n * LN + 1)
                pause(dve, k)
                for t in range(NB):
                    ins = dve.bn_aggr(mv[:, t, :], st[:, t, :])
                ins.then_inc(ln_steps, 1)
                dve.wait_ge(ln_steps, n * LN + 2)
                dve.tensor_scalar(veps[:], mv[:, :, 1], EPS, None, ALU.add).then_inc(ln_steps, 1)
                dve.wait_ge(rstd_done, n + 1)
                for t in range(NB):
                    ins = dve.tensor_scalar((xn, xn2)[r][:, t, :], src(t), mv[:, t, 0:1], rstd[:, t:t + 1],
                                            ALU.subtract, ALU.mult)
                ins.then_inc(ln_steps, 1)
                dve.wait_ge(ln_steps, n * LN + 4)

            def ln(b, _, h, use):
                dve.wait_ge(x_h_done, HALF * b + h + 1)
                dve.tensor_tensor(x_l[:, h * G:(h + 1) * G], xt[:, h, :], x_h[:, h * G:(h + 1) * G].bitcast(F32),
                                  ALU.subtract).then_inc(x_l_done, 1)

            def proj(b, v, h, use):
                base = (HALF * 2 * b + 2 * h + v // 2 + 1) * ROT
                was_read(dve, b, use)
                q = v % 2
                dve.tensor_scalar(head[:, q, :], act_s[:, q, :], par[:, v, 1:2], par[:, v, 2:3], ALU.mult, ALU.add)\
                   .then_inc(rot, 1)
                if q == 0:
                    return
                cut = slice(h * G, (h + 1) * G)
                dve.wait_ge(rot, base + 1)
                dve.tensor_tensor(turned_s[:, 0, :], head[:, 0, :], cos[:, cut], ALU.mult).then_inc(rot, 1)
                dve.wait_ge(rot, base + 2)
                dve.tensor_tensor(turned_s[:, 1, :], head[:, 1, :], sin[:, cut], ALU.mult).then_inc(rot, 1)
                dve.wait_ge(rot, base + 4)
                dve.tensor_tensor(stack[:, v // 2, cut], turned_s[:, 0, :], turned_s[:, 1, :], ALU.add).then_inc(rot, 1)
                dve.wait_ge(rot, base + 5)

            def attn(b, _, h, use):
                bank, empty = content(dve, b, use)
                dve.scalar_tensor_tensor(att_s[:, h, :].rearrange("p (t i) -> p t i", t=TG),
                                         bank.rearrange("p (t i) -> p t i", t=TG), 1.0 / SPAN,
                                         rel[:].unsqueeze(1).broadcast_to([P, TG, P]), ALU.mult, ALU.add)\
                   .then_inc(empty, 1)
                was_read(dve, b, use)
                dve.scalar_tensor_tensor(att[:, h, :], att_s[:, h, :], 0.0, att_s[:, h, :], ALU.max, ALU.mult)\
                   .then_inc(att_steps, 2)

            def out(b, c, h, use):
                bank, empty = content(dve, b, use)
                dve.tensor_tensor(mixed[:, h, c, :], bank, gate[:, c, h * G:(h + 1) * G], ALU.mult).then_inc(empty, 1)

            def ys(b, _, h, use):
                bank, empty = content(dve, b, use)
                base = (HALF * b + h) * YS
                xs = k.x[:, bass.ds(b * S + h * G, G)].rearrange("p (t d) -> p t d", d=D)

                def wide(v):
                    return v[:].unsqueeze(1).broadcast_to([P, TG, D])

                dve.tensor_tensor(y[:, h], bank.rearrange("p (t d) -> p t d", d=D), wide(bo), ALU.add).then_inc(empty, 1)
                was_read(dve, b, use)
                for t in range(TG):
                    ins = dve.bn_stats(st2[:, h, t, :], y[:, h, t, :])
                ins.then_inc(y_steps, 1)
                dve.wait_ge(y_steps, base + 1)
                pause(dve, k)
                for t in range(TG):
                    ins = dve.bn_aggr(mv2[:, h, t, :], st2[:, h, t, :])
                ins.then_inc(y_steps, 1)
                dve.wait_ge(y_steps, base + 2)
                dve.tensor_scalar(veps2[:, h, :], mv2[:, h, :, 1], EPS, None, ALU.add).then_inc(y_steps, 2)
                dve.wait_ge(rstd2_done, HALF * b + h + 1)
                for t in range(TG):
                    ins = dve.tensor_scalar(yn[:, h, t, :], y[:, h, t, :], mv2[:, h, t, 0:1], rstd2[:, h, t:t + 1],
                                            ALU.subtract, ALU.mult)
                ins.then_inc(y_steps, 1)
                dve.wait_ge(y_steps, base + 5)
                dve.tensor_tensor(y[:, h], yn[:, h], wide(ln2w), ALU.mult).then_inc(y_steps, 1)
                dve.wait_ge(y_steps, base + 6)
                dve.tensor_tensor(yn[:, h], y[:, h], wide(ln2b), ALU.add).then_inc(y_steps, 1)
                dve.wait_ge(y_steps, base + 7)
                dve.tensor_tensor(xs, xs, yn[:, h], ALU.add).then_inc(y_steps, 1)
                dve.wait_ge(y_steps, base + 8)

            for q in range(NBANK):
                dve.tensor_copy(flag[:, 2 + q:3 + q], k.ident[:, 0:1]).then_inc(emptied[q], 1)
            dve.tensor_copy(flag[:, 2 + NBANK:3 + NBANK], k.ident[:, 0:1]).then_inc(rot, ROT)
            walk(dve, dict(norm=norm, ln=ln, proj=proj, att=attn, out=out, y=ys))


def phase_store(nc, k, out):
    with ExitStack() as ctx:
        stored = ctx.enter_context(nc.semaphore("stored"))
        block = ctx.enter_context(nc.Block())

        @block.sync
        def _(sp):
            sp.dma_start(out.rearrange("b (n p) d -> p (b n) d", p=P),
                         k.x[:].rearrange("p (n d) -> p n d", d=D)).then_inc(stored, 16)
            sp.wait_ge(stored, 16)


def build(nc, a, out, phases=("ffn0a", "att", "ffn0b", "ffn1a", "gau", "ffn1b")):
    k = Core()
    lay, npack = pack_layout()
    with ExitStack() as ctx:
        def sb(name, shape, dt=F32):
            return ctx.enter_context(nc.sbuf_tensor(name, shape, dt))

        k.x = sb("x", [P, NT * D])
        k.pack = sb("pack", [P, lay["sel0"][0]])
        k.const = lambda name: k.pack[:, lay[name][0]:lay[name][1]]
        k.ident = k.const("ident")
        k.rth, k.rtl = sb("rth", [P, P], F32R), sb("rtl", [P, P], F32R)
        k.gate_bias = sb("gate_bias", [P, E0])
        k.neghalf = sb("neghalf", [P, 8])
        k.banks = ctx.enter_context(nc.psum_tensor("banks", [P, 8, 512], F32))
        k.unread, k.unread_pool = sb("unread", [P, 1]), sb("unread_pool", [32, 1])
        for layer in range(2):
            with ExitStack() as own:
                NC, NSEL = (C0, C0) if layer == 0 else (C1, E1)

                def ws(name, n, dt=F32R):
                    return own.enter_context(nc.sbuf_tensor(f"{name}{layer}", [P, n * P], dt))

                k.wgh, k.wgl, k.wuh, k.wul = ws("wgh", NC), ws("wgl", NC), ws("wuh", NC), ws("wul", NC)
                k.wdt, k.sel = ws("wdt", NC, F32), ws("sel", NSEL)
                phase_setup(nc, k, a, layer)
                k.moe_sems, k.for_layer, turns = {}, own.enter_context, 0
                for name in (("ffn0a", "att", "ffn0b"), ("ffn1a", "gau", "ffn1b"))[layer]:
                    if name not in phases:
                        continue
                    if name == "att":
                        phase_attention(nc, k, a)
                    elif name == "gau":
                        phase_gated(nc, k, a)
                    else:
                        phase_moe(nc, k, name, layer, turns)
                        turns += 1
        phase_store(nc, k, out)


_INS = ['L0_attn_x', 'L0_attn_w_in', 'L0_attn_b_in', 'L0_attn_w_out', 'L0_attn_b_out', 'L0_ffn_gate_w',
        'L0_ffn_gate_bias', 'L0_ffn_w1', 'L0_ffn_w2', 'L0_ffn_w3', 'L0_ffn_ws1', 'L0_ffn_ws2', 'L0_ffn_ws3',
        'L1_attn_ln1_w', 'L1_attn_ln1_b', 'L1_attn_Wqk', 'L1_attn_bqk', 'L1_attn_Wv', 'L1_attn_bv', 'L1_attn_Wg',
        'L1_attn_bg', 'L1_attn_Wo', 'L1_attn_bo', 'L1_attn_ln2_w', 'L1_attn_ln2_b', 'L1_attn_gamma',
        'L1_attn_beta', 'L1_attn_pos_emb', 'L1_ffn_router_w', 'L1_ffn_w_gate', 'L1_ffn_w_up', 'L1_ffn_w_down']


def kernel(**inputs):
    import numpy as _np
    import concourse.bacc as _bacc
    from concourse import mybir as _mybir
    from concourse.bass_utils import run_bass_kernel_spmd as _run

    nc = _bacc.Bacc("TRN2", target_bir_lowering=False, num_devices=1)
    arrays, args = {}, {}
    for name in _INS + ["consts"]:
        x = constants() if name == "consts" else _np.ascontiguousarray(inputs[name])
        arrays[f"in_{name}_dram"] = x
        args[name] = nc.dram_tensor(f"in_{name}_dram", x.shape, _mybir.dt.from_np(x.dtype), kind="ExternalInput").ap()
    out = nc.dram_tensor("out_0_dram", (B, S, D), _mybir.dt.float32, kind="ExternalOutput").ap()
    build(nc, args, out)
    r = _run(nc, [arrays], core_ids=[0])
    return r.results[0]["out_0_dram"]
```

```python
from contextlib import ExitStack

import numpy as np
import concourse.bass as bass
from concourse import mybir

F32 = mybir.dt.float32
F32R = mybir.dt.float32r
BF16 = mybir.dt.bfloat16
ALU = mybir.AluOpType
ACT = mybir.ActivationFunctionType
AX = mybir.AxisListType

P = 128
D = 128
B, S = 4, 1024
T = B * S
NT = T // P
G = 512
NG = T // G
TG = G // P
EPS = 1e-5

E0, I0 = 16, 64
C0 = (E0 + 2) * I0 // P
E1, I1 = 8, 256
C1 = E1 * I1 // P

H, DH = 16, 8
HG = 4
SPAN = 64
QK, HV = 32, 256
NPOS = 33

PAD = -2e30
OUT = -1e30
TAKEN = -3e30


def pack_layout():
    at, lay = 0, {}
    for name, n in (("ident", P), ("causal", P), ("causalT", P), ("qsign", 1), ("qlow", 1), ("ksign", 1),
                    ("klow", 1), ("dist", P), ("outside", P), ("sel0", C0 * P), ("sel1", E1 * P),
                    ("dval", NPOS), ("cos", S), ("sin", S)):
        lay[name] = (at, at + n)
        at += n
    return lay, at


def constants():
    lay, n = pack_layout()
    c = np.zeros((P, n), np.float32)

    def put(name):
        a, b = lay[name]
        return c[:, a:b]

    put("ident")[:] = np.eye(P)
    s0, s1 = put("sel0"), put("sel1")
    for m in range(C0 * P):
        e = m // I0
        if e <= E0:
            s0[e, m] = s0[32 + e, m] = 1
    for e in range(E1):
        s1[e, e * P:(e + 1) * P] = s1[32 + e, e * P:(e + 1) * P] = 1
    i = np.arange(P)
    put("causal")[:] = np.where(i[None, :] > i[:, None], OUT, 0)
    put("causalT")[:] = np.where(i[:, None] > i[None, :], OUT, 0)
    r = i % 32
    qlow, klow = (r >= 8) & (r < 16), (r >= 16) & (r < 24)
    put("qlow")[:, 0], put("klow")[:, 0] = qlow, klow
    put("qsign")[:, 0], put("ksign")[:, 0] = 1 - 2 * qlow, 1 - 2 * klow
    same = (i[:, None] // SPAN) == (i[None, :] // SPAN)
    put("dist")[:] = np.where(same, np.minimum(np.abs(i[:, None] - i[None, :]), NPOS - 1), -1)
    put("outside")[:] = np.where(same, 0, OUT)
    put("dval")[:] = np.arange(NPOS)
    half = QK // 2
    inv = (np.float32(10000.0) ** (-np.arange(half, dtype=np.float32) / np.float32(half))).astype(np.float32)
    ang = np.arange(S, dtype=np.float32)[None, :] * inv[:, None]
    put("cos")[:] = np.tile(np.cos(ang), (P // half, 1))
    put("sin")[:] = np.tile(np.concatenate([-np.sin(ang), np.sin(ang)]), (P // QK, 1))
    return c


def pause(dve, k):
    dve.memset(k.unread[:], 0.0)


class Core:
    pass


def phase_setup(nc, k, a, layer):
    first = layer == 0
    NC, NSEL = (C0, C0) if first else (C1, E1)
    lay, npack = pack_layout()
    with ExitStack() as ctx:
        def sb(name, shape, dt=F32):
            return ctx.enter_context(nc.sbuf_tensor(f"{name}{layer}", shape, dt))

        def sem(name):
            return ctx.enter_context(nc.semaphore(name))

        raw = sb("raw", [P, 3, NC * P])
        sel_raw = sb("sel_raw", [P, NSEL * P])
        router_raw = sb("router_raw", [P, P])
        turn = k.banks[:, 0:4, :]

        def sem(name):
            return ctx.enter_context(nc.semaphore(f"setup{layer}_{name}"))

        consts_in, x_in, cleared, small_in = sem("consts_in"), sem("x_in"), sem("cleared"), sem("small_in")
        w_in = [sem(f"w_in{n}") for n in range(3)]
        turned, high_done, low_done = sem("turned"), sem("high_done"), sem("low_done")

        jobs = []
        for w, dst in ((0, (k.wgh, k.wgl)), (1, (k.wuh, k.wul)), (2, (k.wdh, k.wdl))):
            for c in range(0, NC, 4):
                jobs.append((w, c, min(4, NC - c), dst))
        N = len(jobs)

        block = ctx.enter_context(nc.Block())

        @block.sync
        def _(sp):
            if first:
                sp.dma_start(k.pack[:], a["consts"][:, 0:k.pack.shape[1]]).then_inc(consts_in, 16)
            sp.dma_start(sel_raw[:], a["consts"][:, slice(*lay["sel0" if first else "sel1"])]).then_inc(consts_in, 16)
            sp.wait_ge(cleared, 1)
            if first:
                for w, name in ((0, "w1"), (1, "w3")):
                    sp.dma_start(raw[:, w, 0:8 * P].rearrange("p (c d) -> p c d", d=D),
                                 a["L0_ffn_" + name].rearrange("(c e) i d -> (e i) c d", e=2)).then_inc(w_in[w], 16)
                    sp.dma_start(raw[0:I0, w, 8 * P:9 * P], a["L0_ffn_ws" + name[1]]).then_inc(w_in[w], 16)
                sp.dma_start(raw[:, 2, 0:8 * P].rearrange("p (e i) -> p e i", i=I0),
                             a["L0_ffn_w2"].rearrange("e d i -> d e i")).then_inc(w_in[2], 16)
                sp.dma_start(raw[:, 2, 8 * P:8 * P + I0], a["L0_ffn_ws2"]).then_inc(w_in[2], 16)
            else:
                for w, name in ((0, "w_gate"), (1, "w_up")):
                    sp.dma_start(raw[:, w, :].rearrange("p (c d) -> p c d", d=D),
                                 a["L1_ffn_" + name].rearrange("e (c p) d -> p (e c) d", p=P)).then_inc(w_in[w], 16)
                sp.dma_start(raw[:, 2, :].rearrange("p (e i) -> p e i", i=I1),
                             a["L1_ffn_w_down"].rearrange("e d i -> d e i")).then_inc(w_in[2], 16)

        @block.scalar
        def _(act):
            if first:
                act.dma_start(k.x[:].rearrange("p (n d) -> p n d", d=D),
                              a["L0_attn_x"].rearrange("b (n p) d -> p (b n) d", p=P)).then_inc(x_in, 16)
            for n, (_, c, m, (high, _)) in enumerate(jobs):
                act.wait_ge(turned, n + 1)
                act.activation(high[:, c * P:(c + m) * P], turn[:, n % 4, 0:m * P], ACT.Copy).then_inc(high_done, 1)
            act.wait_ge(turned, N + 1)
            act.activation(k.rth[:], turn[:, N % 4, 0:P], ACT.Copy).then_inc(high_done, 1)
            if first:
                act.wait_ge(x_in, 16)

        @block.gpsimd
        def _(pool):
            pool.memset(router_raw[:], 0.0)
            if first:
                pool.memset(raw[:, :, 8 * P:9 * P], 0.0)
            pool.memset(k.neghalf[:], -0.5).then_inc(cleared, 1)
            pool.wait_ge(cleared, 1)
            router = a["L0_ffn_gate_w" if first else "L1_ffn_router_w"]
            pool.dma_start(router_raw[0:router.shape[0], :], router).then_inc(small_in, 16)
            pool.dma_start(k.gate_bias[:], a["L0_ffn_gate_bias"].partition_broadcast(P)).then_inc(small_in, 16)

        @block.tensor
        def _(pe):
            pe.wait_ge(consts_in, 32 if first else 16)
            for n, (w, c, m, _) in enumerate(jobs):
                pe.wait_ge(w_in[w], 32 if first else 16)
                if n >= 4:
                    pe.wait_ge(high_done, n - 3)
                    pe.wait_ge(low_done, n - 3)
                for j in range(m):
                    mm = pe.transpose(turn[:, n % 4, j * P:(j + 1) * P], raw[:, w, (c + j) * P:(c + j + 1) * P],
                                      k.ident)
                mm.then_inc(turned, 1)
            pe.wait_ge(small_in, 32)
            pe.wait_ge(high_done, N - 3)
            pe.wait_ge(low_done, N - 3)
            pe.transpose(turn[:, N % 4, 0:P], router_raw[:], k.ident).then_inc(turned, 1)

        @block.vector
        def _(dve):
            for n, (_, c, m, (high, low)) in enumerate(jobs):
                dve.wait_ge(high_done, n + 1)
                dve.tensor_tensor(low[:, c * P:(c + m) * P], turn[:, n % 4, 0:m * P],
                                  high[:, c * P:(c + m) * P].bitcast(F32), ALU.subtract).then_inc(low_done, 1)
            dve.wait_ge(consts_in, 32 if first else 16)
            dve.tensor_copy(k.sel[:], sel_raw[:])
            dve.wait_ge(high_done, N + 1)
            dve.tensor_tensor(k.rtl[:], turn[:, N % 4, 0:P], k.rth[:].bitcast(F32), ALU.subtract)


def phase_moe(nc, k, tag, layer, turn_no):
    first = layer == 0
    NC = C0 if first else C1
    NE = E0 if first else E1
    gate_h, gate_l, up_h, up_l, down_h, down_l, sel = k.wgh, k.wgl, k.wuh, k.wul, k.wdh, k.wdl, k.sel

    PER = 1 if first else I1 // P

    def comb_bank(q, c):
        return (q * NC + c) // PER % 2

    g0 = turn_no * NG

    def rows(g):
        return (g - g0) * G

    with ExitStack() as ctx:
        def sem(name):
            if name not in k.moe_sems:
                k.moe_sems[name] = k.for_layer(nc.semaphore(f"moe{layer}_{name}"))
            return k.moe_sems[name]

        def sb(name, shape, dt=F32):
            return ctx.enter_context(nc.sbuf_tensor(f"{tag}_{name}", shape, dt))

        st, mv, veps, rstd = sb("st", [P, TG, 6]), sb("mv", [P, TG, 2]), sb("veps", [P, TG]), sb("rstd", [P, TG])
        xn, xh_sb, xl_sb = sb("xn", [P, TG, D]), sb("xh", [P, 2, G], F32R), sb("xl", [P, 2, G], F32R)
        logits, th, sig, comb = (sb("logits", [P, G]), sb("th", [P, TG, NE]), sb("sig", [P, TG, NE]),
                                 sb("comb", [P, TG, NE]))
        ext, mark = sb("ext", [P, TG, NE + 8]), sb("mark", [P, TG, NE + 8])
        gext, gmark = sb("gext", [P, TG, 12]), sb("gmark", [P, TG, 12])
        top_sb, pen, hs, df = (sb("top", [P, TG, 8]), sb("pen", [P, TG, 4]), sb("hs", [P, TG, 1]),
                               sb("df", [P, TG, E1]))
        cstack, combt = sb("cstack", [P, TG, P]), sb("combt", [P, 2, G], F32R)
        sil, scl, hid = sb("sil", [P, 2, G]), sb("scl", [P, 2, G]), sb("hid", [P, 2, G])
        hid_h, hid_l, y_t = sb("hid_h", [P, 2, G], F32R), sb("hid_l", [P, 2, G], F32R), sb("y_t", [P, G])

        gate_ps, up_ps, comb_ps = k.banks[:, 0:2, :], k.banks[:, 2:4, :], k.banks[:, 4:6, :]
        y_ps, misc = k.banks[:, 6, :], k.banks[:, 7, :]
        misc3 = misc[:].rearrange("p (t c) -> p t c", c=P)

        stats_done, aggr_done, eps_done, rstd_done, norm_done = (sem(s) for s in
            ("stats_done", "aggr_done", "eps_done", "rstd_done", "norm_done"))
        xt_turned, xh_done, xl_done = sem("xt_turned"), sem("xh_done"), sem("xl_done")
        logits_t, logits_out, logits_turned, logits_read = (sem(s) for s in
            ("logits_t", "logits_out", "logits_turned", "logits_read"))
        route = sem("route")
        tanh_done = sem("tanh_done")
        comb_turned, comb_t = sem("comb_turned"), sem("comb_t")
        y_out, y_turned, y_added = sem("y_out"), sem("y_turned"), sem("y_added")
        gate_done, up_done, silu_done, scaled, hidden = (sem(s) for s in
            ("gate_done", "up_done", "silu_done", "scaled", "hidden"))
        high_cut, low_cut, down_done = sem("high_cut"), sem("low_cut"), sem("down_done")
        comb_done, comb_high, stack_cleared = sem("comb_done"), sem("comb_high"), sem("stack_cleared")
        ROUTE = 12 if first else 8

        if first:
            slot = dict(stats=0, aggr=0, rstd=0, norm=1, turn=2, xh=2, xl=2, logit=3, lout=3, lturn=4,
                        r1=4, r2=5, r3=6, r4=7, cturn=8, yout=2, yturn=6, y=7)
        else:
            slot = dict(stats=0, aggr=0, rstd=0, norm=2, turn=3, xh=3, xl=3, logit=5, lout=5, lturn=7,
                        r1=7, r2=9, r3=11, r4=13, cturn=14, yout=2, yturn=9, y=10)

        block = ctx.enter_context(nc.Block())

        @block.tensor
        def _(pe):
            def turn(g, q):
                pe.wait_ge(norm_done, g + 1)
                if not isinstance(g, int) or g > 0:
                    pe.wait_ge(comb_t, g)
                for t in range(TG):
                    mm = pe.transpose(misc[:, t * P:(t + 1) * P], xn[:, t, :], k.ident)
                mm.then_inc(xt_turned, 1)

            def logit(g, q):
                pe.wait_ge(xl_done, g + 1)
                pe.matmul(misc[:], k.rth[:], xh_sb[:, q, :], start=True, stop=False)
                pe.matmul(misc[:], k.rth[:], xl_sb[:, q, :], start=False, stop=False)
                pe.matmul(misc[:], k.rtl[:], xh_sb[:, q, :], start=False, stop=True).then_inc(logits_t, 1)

            def lturn(g, q):
                pe.wait_ge(logits_out, g + 1)
                for t in range(TG):
                    mm = pe.transpose(misc[:, t * P:(t + 1) * P], logits[:, t * P:(t + 1) * P], k.ident)
                mm.then_inc(logits_turned, 1)

            def cturn(g, q):
                pe.wait_ge(route, (g + 1) * ROUTE)
                for t in range(TG):
                    mm = pe.transpose(misc[:, t * P:(t + 1) * P], cstack[:, t, :], k.ident)
                mm.then_inc(comb_turned, 1)

            def up_and_gate(g, q, c):
                n = (q * NC + c) % 2
                num = g * NC + c
                if not (isinstance(num, int) and num < 2):
                    pe.wait_ge(silu_done, num - 1)
                ws = slice(c * P, (c + 1) * P)
                for m, (w, xx) in enumerate(((gate_h, xh_sb), (gate_h, xl_sb), (gate_l, xh_sb))):
                    mm = pe.matmul(gate_ps[:, n, :], w[:, ws], xx[:, q, :], start=m == 0, stop=m == 2)
                mm.then_inc(gate_done, 1)
                if not (isinstance(num, int) and num < 2):
                    pe.wait_ge(hidden, num - 1)
                for m, (w, xx) in enumerate(((up_h, xh_sb), (up_h, xl_sb), (up_l, xh_sb))):
                    mm = pe.matmul(up_ps[:, n, :], w[:, ws], xx[:, q, :], start=m == 0, stop=m == 2)
                if c % PER == 0:
                    e = c // PER
                    if c == 0:
                        pe.wait_ge(comb_t, g + 1)
                    mm = pe.matmul(comb_ps[:, comb_bank(q, c), :], sel[:, e * P:(e + 1) * P], combt[:, q, :],
                                   start=True, stop=True)
                mm.then_inc(up_done, 1)

            def project(g, q, c):
                n = (q * NC + c) % 2
                ws = slice(c * P, (c + 1) * P)
                if c == 0 and not (isinstance(g, int) and g == 0):
                    pe.wait_ge(y_out, g)
                pe.wait_ge(low_cut, g * NC + c + 1)
                pe.matmul(y_ps, down_h[:, ws], hid_h[:, n, :], start=c == 0, stop=False)
                pe.matmul(y_ps, down_l[:, ws], hid_h[:, n, :], start=False, stop=False)
                pe.matmul(y_ps, down_h[:, ws], hid_l[:, n, :], start=False, stop=c == NC - 1).then_inc(down_done, 1)

            def yturn(g, more):
                pe.wait_ge(y_out, g + 1)
                if more:
                    if first:
                        pe.wait_ge(tanh_done, g + 3)
                    else:
                        pe.wait_ge(route, (g + 2) * ROUTE + 1)
                for t in range(TG):
                    mm = pe.transpose(misc[:, t * P:(t + 1) * P], y_t[:, t * P:(t + 1) * P], k.ident)
                mm.then_inc(y_turned, 1)

            def body(g, q, more):
                start = isinstance(g, int) and g == g0
                for c in range(NC):
                    if not (isinstance(g, int) and g < g0):
                        up_and_gate(g, q, c)
                        if c >= 2:
                            project(g, q, c - 2)
                        elif not start:
                            project(g - 1, 1 - q, NC - 2 + c)
                        if slot["yturn"] == c and not start:
                            yturn(g - 1, more)
                    if more:
                        for s, f in (("turn", turn), ("logit", logit), ("lturn", lturn), ("cturn", cturn)):
                            if slot[s] == c:
                                f(g + 1, 1 - q)
            body(g0 - 1, 1, True)
            body(g0, 0, True)
            body(g0 + 1, 1, True)
            with pe.Fori(1, NG // 2 - 1) as i:
                body(g0 + 2 * i, 0, True)
                body(g0 + 2 * i + 1, 1, True)
            body(g0 + NG - 2, 0, True)
            body(g0 + NG - 1, 1, False)
            project(g0 + NG - 1, 1, NC - 2)
            project(g0 + NG - 1, 1, NC - 1)
            pe.wait_ge(y_added, g0 + NG - 1)
            yturn(g0 + NG - 1, False)

        @block.scalar
        def _(act):
            def xh(g, q):
                act.wait_ge(xt_turned, g + 1)
                if not (isinstance(g, int) and g < 2):
                    act.wait_ge(up_done, (g - 1) * NC)
                act.activation(xh_sb[:, q, :], misc[:], ACT.Copy).then_inc(xh_done, 1)

            def lout(g, q):
                act.wait_ge(logits_t, g + 1)
                act.activation(logits[:], misc[:], ACT.Copy).then_inc(logits_out, 1)

            def r1(g, q):
                if first:
                    act.wait_ge(logits_turned, g + 1)
                    act.activation(th[:, :, 0:NE], misc3[:, :, 0:NE], ACT.Tanh, scale=0.5).then_inc(tanh_done, 1)

            def r2(g, q):
                if not first:
                    act.wait_ge(route, g * ROUTE + 4)
                    act.activation(th[:, :, 0:NE], df[:, :, 0:NE], ACT.Tanh).then_inc(tanh_done, 1)

            def cturn(g, q):
                act.wait_ge(comb_turned, g + 1)
                act.activation(combt[:, q, :], misc[:], ACT.Copy).then_inc(comb_t, 1)

            def silu(g, q, c):
                n = (q * NC + c) % 2
                num = g * NC + c
                act.wait_ge(gate_done, num + 1)
                if not (isinstance(num, int) and num < 2):
                    act.wait_ge(scaled, num - 1)
                act.activation(sil[:, n, :], gate_ps[:, n, :], ACT.Silu).then_inc(silu_done, 1)

            def high(g, q, c):
                n = (q * NC + c) % 2
                num = g * NC + c
                act.wait_ge(hidden, num + 1)
                if not (isinstance(num, int) and num < 2):
                    act.wait_ge(down_done, num - 1)
                act.activation(hid_h[:, n, :], hid[:, n, :], ACT.Copy).then_inc(high_cut, 1)

            def yout(g):
                act.wait_ge(down_done, (g + 1) * NC)
                if not (isinstance(g, int) and g == 0):
                    act.wait_ge(y_turned, g)
                act.activation(y_t[:], y_ps, ACT.Copy).then_inc(y_out, 1)

            def body(g, q, more):
                start = isinstance(g, int) and g == g0
                for c in range(NC):
                    if not (isinstance(g, int) and g < g0):
                        if slot["yout"] == c and not start:
                            yout(g - 1)
                        silu(g, q, c)
                        if c > 0:
                            high(g, q, c - 1)
                        elif not start:
                            high(g - 1, 1 - q, NC - 1)
                    if more:
                        for s, f in (("xh", xh), ("lout", lout), ("r1", r1), ("r2", r2), ("cturn", cturn)):
                            if slot[s] == c:
                                f(g + 1, 1 - q)
            body(g0 - 1, 1, True)
            body(g0, 0, True)
            body(g0 + 1, 1, True)
            with act.Fori(1, NG // 2 - 1) as i:
                body(g0 + 2 * i, 0, True)
                body(g0 + 2 * i + 1, 1, True)
            body(g0 + NG - 2, 0, True)
            body(g0 + NG - 1, 1, False)
            high(g0 + NG - 1, 1, NC - 1)
            yout(g0 + NG - 1)

        @block.gpsimd
        def _(pool):
            def invert(g):
                pool.wait_ge(eps_done, g + 1)
                pool.tensor_tensor(rstd[:], veps[:], k.neghalf[:, 0:TG], ALU.pow).then_inc(rstd_done, 1)

            def low(g, q, c):
                n = (q * NC + c) % 2
                num = g * NC + c
                pool.wait_ge(high_cut, num + 1)
                pool.tensor_tensor(hid_l[:, n, :], hid[:, n, :], hid_h[:, n, :].bitcast(F32), ALU.subtract)\
                    .then_inc(low_cut, 1)

            def body(g, q, more):
                start = isinstance(g, int) and g == g0
                for c in range(NC):
                    if c > 0:
                        low(g, q, c - 1)
                    elif not start:
                        low(g - 1, 1 - q, NC - 1)
                    if more and slot["rstd"] == c:
                        invert(g + 1)

            invert(g0)
            body(g0, 0, True)
            body(g0 + 1, 1, True)
            with pool.Fori(1, NG // 2 - 1) as i:
                body(g0 + 2 * i, 0, True)
                body(g0 + 2 * i + 1, 1, True)
            body(g0 + NG - 2, 0, True)
            body(g0 + NG - 1, 1, False)
            low(g0 + NG - 1, 1, NC - 1)

        @block.vector
        def _(dve):
            def stats(g, q):
                for t in range(TG):
                    ins = dve.bn_stats(st[:, t, :], k.x[:, bass.ds(rows(g) + t * P, P)])
                ins.then_inc(stats_done, 1)

            def aggr(g, q):
                dve.wait_ge(stats_done, g + 1)
                pause(dve, k)
                for t in range(TG):
                    ins = dve.bn_aggr(mv[:, t, :], st[:, t, :])
                ins.then_inc(aggr_done, 1)
                dve.wait_ge(aggr_done, g + 1)
                dve.tensor_scalar(veps[:], mv[:, :, 1], EPS, None, ALU.add).then_inc(eps_done, 1)

            def norm(g, q):
                dve.wait_ge(rstd_done, g + 1)
                for t in range(TG):
                    ins = dve.tensor_scalar(xn[:, t, :], k.x[:, bass.ds(rows(g) + t * P, P)], mv[:, t, 0:1],
                                            rstd[:, t:t + 1], ALU.subtract, ALU.mult)
                ins.then_inc(norm_done, 1)

            def xl(g, q):
                dve.wait_ge(xh_done, g + 1)
                dve.tensor_tensor(xl_sb[:, q, :], misc[:], xh_sb[:, q, :].bitcast(F32), ALU.subtract)\
                   .then_inc(xl_done, 1)

            count = [0]

            def step(ins, g):
                count[0] += 1
                ins.then_inc(route, 1)
                dve.wait_ge(route, g * ROUTE + count[0])

            def top(g, width, dst):
                pause(dve, k)
                for t in range(TG):
                    ins = dve.max(dst[:, t, :], width[:, t, :])
                return ins

            def r1(g, q):
                count[0] = 0
                if first:
                    dve.wait_ge(tanh_done, g + 1)
                    step(dve.tensor_scalar(sig[:, :, 0:NE], th[:, :, 0:NE], 0.5, 0.5, ALU.mult, ALU.add), g)
                    step(dve.tensor_tensor(ext[:, :, 0:NE], sig[:, :, 0:NE],
                                           k.gate_bias[:].unsqueeze(1).broadcast_to([P, TG, NE]), ALU.add), g)
                    step(dve.tensor_reduce(gext[:, :, 0:4], ext[:, :, 0:NE].rearrange("p t (g e) -> p t g e", e=4),
                                           AX.X, ALU.max), g)
                else:
                    dve.wait_ge(logits_turned, g + 1)
                    step(dve.tensor_copy(ext[:, :, 0:NE], misc3[:, :, 0:NE]), g)
                    step(top(g, ext, top_sb), g)

            def r2(g, q):
                if first:
                    step(top(g, gext, top_sb), g)
                    step(dve.memset(top_sb[:, :, 2:8], PAD), g)
                    pause(dve, k)
                    for t in range(TG):
                        ins = dve.match_replace(gmark[:, t, :], top_sb[:, t, :], gext[:, t, :], TAKEN)
                    step(ins, g)
                    step(dve.tensor_scalar(pen[:], gmark[:, :, 0:4], TAKEN, OUT, ALU.not_equal, ALU.mult), g)
                else:
                    step(dve.tensor_tensor(hs[:], top_sb[:, :, 0:1], top_sb[:, :, 1:2], ALU.add), g)
                    step(dve.scalar_tensor_tensor(df[:], hs[:].broadcast_to([P, TG, E1]), -0.5,
                                                  ext[:, :, 0:NE], ALU.mult, ALU.add), g)

            def r3(g, q):
                if first:
                    step(dve.tensor_tensor(ext[:, :, 0:NE].rearrange("p t (g e) -> p t g e", e=4),
                                           ext[:, :, 0:NE].rearrange("p t (g e) -> p t g e", e=4),
                                           pen[:].unsqueeze(3).broadcast_to([P, TG, 4, 4]), ALU.add), g)
                    step(top(g, ext, top_sb), g)
                    step(dve.memset(top_sb[:, :, 4:8], PAD), g)
                else:
                    step(dve.memset(top_sb[:, :, 2:8], PAD), g)
                pause(dve, k)
                for t in range(TG):
                    ins = dve.match_replace(mark[:, t, :], top_sb[:, t, :], ext[:, t, :], TAKEN)
                step(ins, g)
                if not first:
                    dve.wait_ge(tanh_done, g + 1)
                    step(dve.tensor_scalar(sig[:, :, 0:NE], th[:, :, 0:NE], 0.5, 0.5, ALU.mult, ALU.add), g)

            def r4(g, q):
                ins = dve.scalar_tensor_tensor(comb[:, :, 0:NE], mark[:, :, 0:NE], TAKEN, sig[:, :, 0:NE],
                                               ALU.is_equal, ALU.mult)
                ins.then_inc(comb_done, 1)
                dve.wait_ge(comb_done, g + 1)
                if not (isinstance(g, int) and g == 0):
                    dve.wait_ge(comb_turned, g)
                dve.tensor_copy(cstack[:, :, 0:NE].bitcast(F32R), comb[:, :, 0:NE]).then_inc(comb_high, 1)
                dve.wait_ge(comb_high, g + 1)
                dve.tensor_tensor(cstack[:, :, 32:32 + NE].bitcast(F32R), comb[:, :, 0:NE],
                                  cstack[:, :, 0:NE], ALU.subtract).then_inc(route, 1)
                count[0] += 1
                assert count[0] == ROUTE, count[0]

            def add(g):
                dve.wait_ge(y_turned, g + 1)
                dve.scalar_tensor_tensor(k.x[:, bass.ds(rows(g), G)], misc, 0.5, k.x[:, bass.ds(rows(g), G)],
                                         ALU.mult, ALU.add).then_inc(y_added, 1)

            def scale(g, q, c):
                n = (q * NC + c) % 2
                num = g * NC + c
                dve.wait_ge(silu_done, num + 1)
                dve.wait_ge(up_done, num + 1)
                dve.tensor_tensor(scl[:, n, :], sil[:, n, :], comb_ps[:, comb_bank(q, c), :], ALU.mult).then_inc(scaled, 1)

            def hide(g, q, c):
                n = (q * NC + c) % 2
                num = g * NC + c
                dve.wait_ge(scaled, num + 1)
                if not (isinstance(num, int) and num < 2):
                    dve.wait_ge(low_cut, num - 1)
                dve.tensor_tensor(hid[:, n, :], scl[:, n, :], up_ps[:, n, :], ALU.mult).then_inc(hidden, 1)

            def body(g, q, more):
                real = not (isinstance(g, int) and g < g0)
                for c in range(NC):
                    if real and slot["y"] == c and not (isinstance(g, int) and g == g0):
                        add(g - 1)
                    if real:
                        scale(g, q, c)
                        hide(g, q, c)
                    if more:
                        for s, f in (("stats", stats), ("aggr", aggr), ("norm", norm), ("xl", xl), ("r1", r1),
                                     ("r2", r2), ("r3", r3), ("r4", r4)):
                            if slot[s] == c:
                                f(g + 1, 1 - q)

            dve.memset(ext[:], PAD)
            dve.memset(gext[:], PAD)
            dve.memset(cstack[:], 0.0).then_inc(stack_cleared, 1)
            dve.wait_ge(stack_cleared, turn_no + 1)
            if first:
                dve.memset(cstack[:, :, E0:E0 + 1], 1.0)
            body(g0 - 1, 1, True)
            body(g0, 0, True)
            body(g0 + 1, 1, True)
            with dve.Fori(1, NG // 2 - 1) as i:
                body(g0 + 2 * i, 0, True)
                body(g0 + 2 * i + 1, 1, True)
            body(g0 + NG - 2, 0, True)
            body(g0 + NG - 1, 1, False)
            add(g0 + NG - 1)


def phase_attention(nc, k, a):
    NB = S // P
    HALF = S // G
    WIDE = [(t, c) for t in range(NB) for c in range(t // TG + 1)]

    def width_of(t, c):
        return min(G, (t + 1) * P - c * G)

    MAXU = [((t, c),) for t, c in WIDE if width_of(t, c) == G]
    thin = sorted((e for e in WIDE if width_of(*e) < G), key=lambda e: width_of(*e))
    MAXU += [(thin[n], thin[-1 - n]) for n in range(len(thin) // 2)]
    assert all(sum(width_of(*e) for e in unit) <= G for unit in MAXU)
    UNITS = [(qg, kb) for qg in range(HALF) for kb in range(TG * (qg + 1))]
    NU = len(UNITS)
    SCALE = float(np.float32(1.0 / np.sqrt(DH)))

    PROJ = [("proj", w, h) for w in range(2) for h in range(HALF)]
    PADS = [("pad", j, 0) for j in range(HG)]
    PEAKS = [("max", j, u) for j in range(HG) for u in range(len(MAXU))]
    NEXT = [("ln", 0, h) for h in range(HALF)] + [("vt", 0, h) for h in range(HALF)]
    FROM, TILL = 1, 10

    def section(hg):
        peaks = list(PEAKS)
        out = [("vtok", 0, h) for h in range(HALF)] if hg == 0 else []
        for u in range(NU):
            back = (u - 1, 0) if u > 0 else (NU - 1, -1)
            slots = [("score", u, j) for j in range(HG)]
            if u > 0 or hg > 0:
                slots += [("pv", back[0], (j, back[1])) for j in range(HG)]
            for n, e in enumerate(slots):
                out.append(e)
                if u == 0 and (n + 1) % (len(slots) // 4) == 0:
                    out.append(PROJ[(n + 1) // (len(slots) // 4) - 1])
                if u == 0 and n == len(slots) - 1:
                    out += PADS
                if FROM <= u < TILL:
                    at = (u - FROM) * 2 * HG + n
                    end = (TILL - FROM) * 2 * HG
                    if len(PEAKS) * (at + 1) // end > len(PEAKS) * at // end:
                        out.append(peaks.pop(0))
            if u == 1 and hg > 0:
                out += [("oevac", 1, -1), ("ot", 1, -1)]
            if hg == 1 and u == 6:
                out.append(("stats", 0, 0))
            if hg == 1 and u == 9:
                out.append(("norm", 0, 0))
            if u == TILL - 1:
                out.append(("maxt", 0, 0))
            if hg == 2 and u == NU - 1:
                out += NEXT
            if u == 5:
                out += [("oevac", 0, 0), ("ot", 0, 0)]
        assert not peaks
        if hg == HG - 1:
            out += [("pv", NU - 1, (j, 0)) for j in range(HG)] + [("oevac", 1, 0), ("ot", 1, 0)]
            out += [("ont", 0, 0), ("ont", 0, 1), ("wo", 0, 0), ("wo", 0, 1)]
        return out

    SHARED = ("proj", "max", "maxt", "ln", "vt", "vtok", "ot", "ont", "wo")
    PREP = PROJ + PADS + PEAKS + [("maxt", 0, 0)]
    PROLOGUE = [("stats", 0, 0), ("norm", 0, 0)] + NEXT + PREP
    N0 = sum(e[0] in SHARED for e in PROLOGUE)
    BODY = [(hg, e) for hg in range(HG) for e in section(hg)]
    NBODY = sum(e[0] in SHARED for _, e in BODY)
    assert NBODY % 2 == 0

    with ExitStack() as ctx:
        def sb(name, shape, dt=F32):
            return ctx.enter_context(nc.sbuf_tensor(f"att_{name}", shape, dt))

        def sem(name):
            return ctx.enter_context(nc.semaphore(f"att_{name}"))

        w_raw, b_raw = sb("w_raw", [P, 4, D]), sb("b_raw", [1, 3 * D])
        wqk_h, wqk_l = sb("wqk_h", [P, 2, H * 32], F32R), sb("wqk_l", [P, 2, H * 32], F32R)
        wv_h, wv_l = sb("wv_h", [P, P], F32R), sb("wv_l", [P, P], F32R)
        wo_t = sb("wo_t", [P, P])
        bqk = sb("bqk", [P, 2, H * 32], F32R)
        ones = sb("ones", [P, G], F32R)
        bv, bo = sb("bv", [P, 1]), sb("bo", [P, D])
        ident_b, causal_b, causal_tb = sb("ident_b", [P, P], BF16), sb("causal_b", [P, P], BF16), \
            sb("causal_tb", [P, P], BF16)
        st, mv, veps, rstd = sb("st", [P, NB, 6]), sb("mv", [P, NB, 2]), sb("veps", [P, NB]), sb("rstd", [P, NB])
        xn = sb("xn", [P, NB, D])
        xn_h, xn_l = sb("xn_h", [P, S], F32R), sb("xn_l", [P, S], F32R)
        signed = sb("signed", [P, 2, G], F32R)
        q_st = sb("q_st", [P, 2, S], F32R)
        k_st = sb("k_st", [P, S], F32R)
        k_pad = sb("k_pad", [P, 2, HG, S], F32R)
        v_t, v_aug = sb("v_t", [P, S]), sb("v_aug", [P, NB, H, 32])
        mx, nm, mst = sb("mx", [P, HG, NB, 2]), sb("nm", [P, HG * NB]), sb("mst", [P, P])
        m_t = sb("m_t", [2 * HG * NB, P])
        probs = sb("probs", [P, 2, HG, G])
        o_sb, rec, o_tok = sb("o_sb", [P, 2, G]), sb("rec", [P, 2, TG, HG, 1]), sb("o_tok", [P, NB, D])
        on_t = sb("on_t", [P, S])
        y, ypos = sb("y", [P, TG, D]), sb("ypos", [P, TG, D])

        score_ps = k.banks[:, 0:4, :].rearrange("p (n h) c -> p n h c", n=2)
        shared, o_ps = k.banks[:, 4:6, :], k.banks[:, 6:8, :]

        w_in, turned, high_done, zeroed, ready = (sem(s) for s in ("w_in", "turned", "high_done", "zeroed", "ready"))
        with nc.Block() as block:
            @block.sync
            def _(sp):
                sp.dma_start(w_raw[:, 0:3, :], a["L0_attn_w_in"].rearrange("(w r) d -> r w d", r=P)).then_inc(w_in, 16)
                sp.dma_start(w_raw[:, 3, :], a["L0_attn_w_out"]).then_inc(w_in, 16)
                sp.dma_start(b_raw[:], a["L0_attn_b_in"].rearrange("(o n) -> o n", o=1)).then_inc(w_in, 16)
                sp.dma_start(bv[:], a["L0_attn_b_in"][2 * D:3 * D].rearrange("(n o) -> n o", o=1)).then_inc(w_in, 16)
                sp.dma_start(bo[:], a["L0_attn_b_out"].partition_broadcast(P)).then_inc(w_in, 16)

            @block.tensor
            def _(pe):
                pe.wait_ge(w_in, 80)
                for w in range(4):
                    mm = pe.transpose(shared[:, 0, w * P:(w + 1) * P], w_raw[:, w, :], k.ident)
                mm.then_inc(turned, 1)

            @block.gpsimd
            def _(pool):
                pool.memset(wqk_h[:].bitcast(F32), 0.0)
                pool.memset(wqk_l[:].bitcast(F32), 0.0)
                pool.memset(bqk[:].bitcast(F32), 0.0).then_inc(zeroed, 1)
                pool.memset(k_pad[:].bitcast(F32), 0.0)
                pool.memset(v_aug[:], 0.0).then_inc(zeroed, 1)
                pool.wait_ge(zeroed, 2)
                pool.memset(v_aug[:, :, :, DH:DH + 1], 1.0)
                pool.memset(mx[:], -3e38)
                pool.memset(mst[:], 0.0)

            @block.scalar
            def _(act):
                act.wait_ge(turned, 1)
                act.wait_ge(zeroed, 1)
                for w in range(2):
                    src = shared[:, 0, w * P:(w + 1) * P].rearrange("p (h d) -> p h d", d=DH)
                    row = b_raw[0:1, w * D:(w + 1) * D].rearrange("p (h d) -> p h d", d=DH)
                    for r in range(3):
                        cut = slice(r * DH, (r + 1) * DH)
                        act.activation(wqk_h[:, w, :].rearrange("p (h c) -> p h c", c=32)[:, :, cut], src, ACT.Copy)
                        act.activation(bqk[0:1, w, :].rearrange("p (h c) -> p h c", c=32)[:, :, cut], row, ACT.Copy)
                act.activation(wv_h[:], shared[:, 0, 2 * P:3 * P], ACT.Copy)
                act.activation(wo_t[:], shared[:, 0, 3 * P:4 * P], ACT.Copy).then_inc(high_done, 1)

            @block.vector
            def _(dve):
                dve.memset(ones[:].bitcast(F32), 1.0)
                dve.tensor_copy(ident_b[:], k.ident)
                dve.tensor_copy(causal_b[:], k.const("causal"))
                dve.tensor_copy(causal_tb[:], k.const("causalT"))
                dve.wait_ge(high_done, 1)
                for w in range(2):
                    src = shared[:, 0, w * P:(w + 1) * P].rearrange("p (h d) -> p h d", d=DH)
                    row = b_raw[0:1, w * D:(w + 1) * D].rearrange("p (h d) -> p h d", d=DH)
                    wh = wqk_h[:, w, :].rearrange("p (h c) -> p h c", c=32)
                    wl = wqk_l[:, w, :].rearrange("p (h c) -> p h c", c=32)
                    b3 = bqk[:, w, :].rearrange("p (h c) -> p h c", c=32)
                    for r in range(3):
                        cut = slice(r * DH, (r + 1) * DH)
                        dve.tensor_tensor(wl[:, :, cut], src, wh[:, :, cut].bitcast(F32), ALU.subtract)
                        dve.tensor_tensor(b3[32:33, :, cut], row, b3[0:1, :, cut].bitcast(F32), ALU.subtract)
                dve.memset(bqk[0:1, 1, :].rearrange("p (h c) -> p h c", c=32)[:, :, 24:26].bitcast(F32), 1.0)
                dve.tensor_tensor(wv_l[:], shared[:, 0, 2 * P:3 * P], wv_h[:].bitcast(F32), ALU.subtract)

        filled = [sem(f"filled{n}") for n in range(2)]
        emptied = [sem(f"emptied{n}") for n in range(2)]
        ln_steps, rstd_done = sem("ln_steps"), sem("rstd_done")
        signed_done, padded, padded_pool = sem("signed_done"), sem("padded"), sem("padded_pool")
        unread = sb("unread", [32, 1])
        neg_steps, max_in = sem("neg_steps"), sem("max_in")
        scored, exped, attended = sem("scored"), sem("exped"), sem("attended")
        o_read, rec_done, y_steps = sem("o_read"), sem("rec_done"), sem("y_steps")
        xh_done, aggr_done = sem("xh_done"), sem("aggr_done")

        def walk(eng, parts):
            def run(entries, b, first):
                use = first
                for hg, (kind, x, z) in entries:
                    if kind in parts:
                        parts[kind](b, hg, x, z, use)
                    if kind in SHARED:
                        use += 1

            run([(-1, e) for e in PROLOGUE], 0, 0)
            with eng.Fori(0, B - 1) as b:
                run(BODY, b, N0)
            last = [(hg, e) for hg, e in BODY if not (hg == HG - 1 and e in PREP) and
                    e[0] not in ("stats", "norm", "ln", "vt")]
            run(last, B - 1, N0)

        def use_of(b, hg, use):
            return use % 2, use // 2 + (b * (NBODY // 2) if hg >= 0 else 0)

        def fill(pe, b, hg, use):
            q, before = use_of(b, hg, use)
            if not (isinstance(before, int) and before == 0):
                pe.wait_ge(emptied[q], before)
            return shared[:, q, :], filled[q]

        def content(eng, b, hg, use):
            q, before = use_of(b, hg, use)
            eng.wait_ge(filled[q], before + 1)
            return shared[:, q, :], emptied[q]

        def nxt(b, hg):
            return (0, 0) if hg < 0 else (b * HG + hg + 1, (hg + 1) % 2)

        block = ctx.enter_context(nc.Block())

        @block.tensor
        def _(pe):
            def ln(b, hg, _, h, use):
                bank, full = fill(pe, b, hg, use)
                n = 0 if hg < 0 else b + 1
                pe.wait_ge(ln_steps, 3 * n + 3)
                for t in range(TG):
                    mm = pe.transpose(bank[:, t * P:(t + 1) * P], xn[:, h * TG + t, :], k.ident)
                mm.then_inc(full, 1)

            def three(bank, full, wh, wl, h, more=None):
                mm = pe.matmul(bank, wh, xn_h[:, h * G:(h + 1) * G], start=True, stop=False)
                mm = pe.matmul(bank, wh, xn_l[:, h * G:(h + 1) * G], start=False, stop=False)
                mm = pe.matmul(bank, wl, xn_h[:, h * G:(h + 1) * G], start=False, stop=more is None)
                if more is not None:
                    mm = pe.matmul(bank, more, ones[:], start=False, stop=True)
                mm.then_inc(full, 1)

            def vt(b, hg, _, h, use):
                bank, full = fill(pe, b, hg, use)
                if h == 0:
                    q, before = use_of(b, hg, use - 1)
                    pe.wait_ge(emptied[q], before + 1)
                three(bank, full, wv_h[:], wv_l[:], h)

            def proj(b, hg, w, h, use):
                bank, full = fill(pe, b, hg, use)
                g = (hg + 1) % HG
                ws = slice(g * P, (g + 1) * P)
                three(bank, full, wqk_h[:, w, ws], wqk_l[:, w, ws], h, bqk[:, w, ws])

            def peak(b, hg, j, u, use):
                bank, full = fill(pe, b, hg, use)
                n, p = nxt(b, hg)
                if u == 0:
                    pe.wait_ge(*((padded, HG // 2 * n + j + 1) if j < HG // 2 else
                                 (padded_pool, HG // 2 * n + j - HG // 2 + 1)))
                at = 0
                for t, c in MAXU[u]:
                    width = width_of(t, c)
                    diag = c == t // TG
                    mm = pe.matmul(bank[:, at:at + width], q_st[:, p, t * P:(t + 1) * P],
                                   k_pad[:, p, j, c * G:c * G + width], start=True, stop=not diag)
                    if diag:
                        mm = pe.matmul(bank[:, at + width - P:at + width], ident_b[:], causal_b[:], start=False, stop=True)
                    at += width
                mm.then_inc(full, 1)

            def maxt(b, hg, _, __, use):
                bank, full = fill(pe, b, hg, use)
                n, p = nxt(b, hg)
                pe.wait_ge(neg_steps, 3 * n + 3)
                pe.transpose(bank[:, 0:P], mst[:], k.ident).then_inc(full, 1)

            def vtok(b, hg, _, h, use):
                bank, full = fill(pe, b, hg, use)
                for t in range(TG):
                    mm = pe.transpose(bank[:, t * P:(t + 1) * P], v_t[:, (h * TG + t) * P:(h * TG + t + 1) * P], k.ident)
                mm.then_inc(full, 1)

            def score(b, hg, u, j, use):
                pair, i = j // 2, j % 2
                p = hg % 2
                qg, kb = UNITS[u]
                r = max(0, kb - TG * qg)
                n = G - r * P
                if u == 0 and j == 0:
                    pe.wait_ge(max_in, 2 * 16 * (b * HG + hg + 1))
                if i == 0:
                    pe.wait_ge(exped, ((b * HG + hg) * NU + u) * 2 + pair + 1)
                mm = pe.matmul(score_ps[:, pair, i, 0:n], k_pad[:, p, j, kb * P:(kb + 1) * P],
                               q_st[:, p, qg * G + r * P:(qg + 1) * G], start=True, stop=kb < TG * qg)
                if kb >= TG * qg:
                    mm = pe.matmul(score_ps[:, pair, i, 0:P], ident_b[:], causal_tb[:], start=False, stop=True)
                if i == 1:
                    mm.then_inc(scored, 1)

            def pv(b, hg, u, part, use):
                j, back = part
                g = hg + back
                num = (b * HG + g) * NU + u
                qg, kb = UNITS[u]
                r = max(0, kb - TG * qg)
                if j == 0:
                    pe.wait_ge(exped, 2 * num + 2 + 2)
                if kb == 0 and j == 0:
                    pe.wait_ge(o_read, 2 * (b * HG + g) + qg + 1)
                    if u == 0 and g == 0:
                        q, before = use_of(b, hg, HALF - 1 + N0)
                        pe.wait_ge(emptied[q], before + 1)
                mm = pe.matmul(o_ps[32 * j:32 * j + 32, qg, r * P:G], v_aug[:, kb, g * HG + j, :],
                               probs[:, u % 2, j, 0:G - r * P], start=kb == 0, stop=kb == TG * (qg + 1) - 1,
                               tile_position=(0, 32 * j), skip_group_check=True)
                if j == HG - 1:
                    mm.then_inc(attended, 1)

            def ot(b, hg, qg, back, use):
                bank, full = fill(pe, b, hg, use)
                pe.wait_ge(o_read, 2 * (b * HG + hg + back) + qg + 3)
                for t in range(TG):
                    mm = pe.transpose(bank[:, t * P:(t + 1) * P], o_sb[:, qg, t * P:(t + 1) * P], k.ident)
                mm.then_inc(full, 1)

            def ont(b, hg, _, h, use):
                bank, full = fill(pe, b, hg, use)
                if h == 0:
                    q, before = use_of(b, hg, use - 1)
                    pe.wait_ge(emptied[q], before + 1)
                for t in range(TG):
                    mm = pe.transpose(bank[:, t * P:(t + 1) * P], o_tok[:, h * TG + t, :], k.ident)
                mm.then_inc(full, 1)

            def wo(b, hg, _, h, use):
                bank, full = fill(pe, b, hg, use)
                for t in range(TG):
                    mm = pe.matmul(bank[:, t * P:(t + 1) * P], on_t[:, (h * TG + t) * P:(h * TG + t + 1) * P], wo_t[:],
                                   start=True, stop=True, skip_group_check=True)
                mm.then_inc(full, 1)

            walk(pe, dict(ln=ln, vt=vt, proj=proj, max=peak, maxt=maxt, vtok=vtok, score=score, pv=pv, ot=ot,
                          ont=ont, wo=wo))

        @block.scalar
        def _(act):
            def ln(b, hg, _, h, use):
                q, before = use_of(b, hg, use)
                act.wait_ge(filled[q], before + 1)
                act.activation(xn_h[:, h * G:(h + 1) * G], shared[:, q, :], ACT.Copy).then_inc(xh_done, 1)

            def vt(b, hg, _, h, use):
                bank, empty = content(act, b, hg, use)
                act.activation(v_t[:, h * G:(h + 1) * G], bank, ACT.Identity, bias=bv[:, 0:1]).then_inc(empty, 1)

            def proj(b, hg, w, h, use):
                q, before = use_of(b, hg, use)
                act.wait_ge(filled[q], before + 1)
                act.activation(signed[:, h % 2, :], shared[:, q, :], ACT.Identity,
                               scale=k.const(("qsign", "ksign")[w])).then_inc(signed_done, 1)

            def maxt(b, hg, _, __, use):
                n, p = nxt(b, hg)
                if not (isinstance(n, int) and n == 0):
                    act.wait_ge(max_in, 2 * 16 * n)
                bank, empty = content(act, b, hg, use)
                act.activation(m_t[:], bank[0:2 * HG * NB, 0:P], ACT.Copy).then_inc(empty, 1)

            def score(b, hg, u, j, use):
                pair = j // 2
                if j % 2 == 1:
                    return
                num = (b * HG + hg) * NU + u
                qg, kb = UNITS[u]
                n = G - max(0, kb - TG * qg) * P
                if pair == 0:
                    act.wait_ge(attended, num + 1)
                act.wait_ge(scored, 2 * num + pair + 1)
                act.activation(probs[:, u % 2, 2 * pair:2 * pair + 2, 0:n], score_ps[:, pair, :, 0:n], ACT.Exp,
                               scale=SCALE).then_inc(exped, 1)

            def pad(b, hg, j, _, use):
                if j >= HG // 2:
                    return
                n, p = nxt(b, hg)
                if j == 0:
                    for half in (use - 2, use - 1):
                        q, before = use_of(b, hg, half)
                        act.wait_ge(emptied[q], before + 1)
                rows = slice(32 * j, 32 * j + 32)
                act.activation(k_pad[rows, p, j, :], k_st[rows, :].bitcast(F32), ACT.Copy).then_inc(padded, 1)

            def oevac(b, hg, qg, back, use):
                g = b * HG + hg + back
                last = UNITS.index((qg, TG * (qg + 1) - 1))
                act.wait_ge(attended, g * NU + last + 1 + 2)
                act.activation(o_sb[:, qg, :], o_ps[:, qg, :], ACT.Copy).then_inc(o_read, 1)

            def ont(b, hg, _, h, use):
                bank, empty = content(act, b, hg, use)
                act.activation(on_t[:, h * G:(h + 1) * G], bank, ACT.Copy).then_inc(empty, 1)

            act.activation(y[:, 0, 0:1], k.ident[:, 0:1], ACT.Copy).then_inc(exped, 2)
            act.activation(y[:, 0, 1:2], k.ident[:, 0:1], ACT.Copy).then_inc(attended, 2)
            act.activation(y[:, 0, 2:3], k.ident[:, 0:1], ACT.Copy).then_inc(o_read, 2)
            walk(act, dict(ln=ln, vt=vt, proj=proj, pad=pad, maxt=maxt, score=score, oevac=oevac, ont=ont))

        @block.gpsimd
        def _(pool):
            def norm(b, hg, _, __, use):
                n = 0 if hg < 0 else b + 1
                if hg >= 0:
                    pool.wait_ge(padded_pool, HG // 2 * (b * HG + hg + 2))
                pool.wait_ge(ln_steps, 3 * n + 2)
                pool.tensor_tensor(rstd[:], veps[:], k.neghalf[:, 0:NB], ALU.pow).then_inc(rstd_done, 1)

            def pad(b, hg, j, _, use):
                if j < HG // 2:
                    return
                n, p = nxt(b, hg)
                if j == HG // 2:
                    for half in (use - 2, use - 1):
                        q, before = use_of(b, hg, half)
                        pool.wait_ge(emptied[q], before + 1)
                    pool.tensor_tensor(unread[:], k.neghalf[0:32, 0:1], k.neghalf[0:32, 0:1], ALU.add)
                rows = slice(32 * j, 32 * j + 32)
                pool.tensor_copy(k_pad[rows, p, j, :], k_st[rows, :].bitcast(F32)).then_inc(padded_pool, 1)

            walk(pool, dict(norm=norm, pad=pad))

        @block.sync
        def _(sp):
            def maxt(b, hg, _, __, use):
                n, p = nxt(b, hg)
                content(sp, b, hg, use)
                q, before = use_of(b, hg, use)
                sp.wait_ge(emptied[q], before + 1)
                for part in range(2):
                    r = part * HG * NB
                    sp.dma_start(q_st[24 + part:P:32, p, :].bitcast(F32), m_t[r:r + HG * NB, :]).then_inc(max_in, 16)

            walk(sp, dict(maxt=maxt))

        @block.vector
        def _(dve):
            def stats(b, hg, _, __, use):
                n = 0 if hg < 0 else b + 1
                for t in range(NB):
                    ins = dve.bn_stats(st[:, t, :], k.x[:, bass.ds(n * S + t * P, P)])
                ins.then_inc(ln_steps, 1)
                dve.wait_ge(ln_steps, 3 * n + 1)
                pause(dve, k)
                for t in range(NB):
                    ins = dve.bn_aggr(mv[:, t, :], st[:, t, :])
                ins.then_inc(aggr_done, 1)
                dve.wait_ge(aggr_done, n + 1)
                dve.tensor_scalar(veps[:], mv[:, :, 1], EPS, None, ALU.add).then_inc(ln_steps, 1)

            def norm(b, hg, _, __, use):
                n = 0 if hg < 0 else b + 1
                dve.wait_ge(rstd_done, n + 1)
                for t in range(NB):
                    ins = dve.tensor_scalar(xn[:, t, :], k.x[:, bass.ds(n * S + t * P, P)], mv[:, t, 0:1],
                                            rstd[:, t:t + 1], ALU.subtract, ALU.mult)
                ins.then_inc(ln_steps, 1)

            def ln(b, hg, _, h, use):
                bank, empty = content(dve, b, hg, use)
                n = 0 if hg < 0 else b + 1
                dve.wait_ge(xh_done, 2 * n + h + 1)
                dve.tensor_tensor(xn_l[:, h * G:(h + 1) * G], bank, xn_h[:, h * G:(h + 1) * G].bitcast(F32),
                                  ALU.subtract).then_inc(empty, 1)

            def proj(b, hg, w, h, use):
                n, p = nxt(b, hg)
                bank, empty = content(dve, b, hg, use)
                dve.wait_ge(signed_done, 4 * n + w * HALF + h + 1)
                dst = (q_st[:, p, :], k_st[:])[w][:, h * G:(h + 1) * G]
                if w == 1 and h == 0 and hg >= 0:
                    dve.wait_ge(padded, HG // 2 * n)
                    dve.wait_ge(padded_pool, HG // 2 * n)
                dve.scalar_tensor_tensor(dst, bank, k.const(("qlow", "klow")[w]), signed[:, h % 2, :].bitcast(F32),
                                         ALU.mult, ALU.add).then_inc(empty, 1)

            def peak(b, hg, j, u, use):
                bank, empty = content(dve, b, hg, use)
                at = 0
                for t, c in MAXU[u]:
                    width = width_of(t, c)
                    ins = dve.tensor_reduce(mx[:, j, t, c:c + 1], bank[:, at:at + width], AX.X, ALU.max)
                    at += width
                ins.then_inc(empty, 1)

            def maxt(b, hg, _, __, use):
                n, p = nxt(b, hg)
                for last in (use - 2, use - 1):
                    q, before = use_of(b, hg, last)
                    dve.wait_ge(emptied[q], before + 1)
                dve.tensor_reduce(nm[:], mx[:].rearrange("p j t c -> p (j t) c"), AX.X, ALU.max, negate=True)\
                   .then_inc(neg_steps, 1)
                dve.wait_ge(neg_steps, 3 * n + 1)
                dve.tensor_copy(mst[:, 0:HG * NB].bitcast(F32R), nm[:]).then_inc(neg_steps, 1)
                dve.wait_ge(neg_steps, 3 * n + 2)
                dve.tensor_tensor(mst[:, HG * NB:2 * HG * NB].bitcast(F32R), nm[:], mst[:, 0:HG * NB], ALU.subtract)\
                   .then_inc(neg_steps, 1)

            def vtok(b, hg, _, h, use):
                bank, empty = content(dve, b, hg, use)
                dve.tensor_copy(v_aug[:, h * TG:(h + 1) * TG, :, 0:DH],
                                bank.rearrange("p (t h d) -> p t h d", h=H, d=DH)).then_inc(empty, 1)

            def ot(b, hg, qg, back, use):
                bank, empty = content(dve, b, hg, use)
                g = hg + back
                o = bank.rearrange("p (t j d) -> p t j d", j=HG, d=32)
                dve.reciprocal(rec[:, qg], o[:, :, :, DH:DH + 1]).then_inc(rec_done, 1)
                dve.wait_ge(rec_done, 2 * (b * HG + g) + qg + 1)
                for t in range(TG):
                    ins = dve.tensor_tensor(o_tok[:, qg * TG + t, g * 32:g * 32 + 32].rearrange("p (j d) -> p j d", d=DH),
                                            o[:, t, :, 0:DH], rec[:, qg, t, :, :].broadcast_to([P, HG, DH]), ALU.mult)
                ins.then_inc(empty, 1)

            def wo(b, hg, _, h, use):
                bank, empty = content(dve, b, hg, use)
                xs = k.x[:, bass.ds(b * S + h * G, G)]
                base = (b * HALF + h) * 4
                dve.tensor_tensor(y[:], bank.rearrange("p (t d) -> p t d", d=D),
                                  bo[:].unsqueeze(1).broadcast_to([P, TG, D]), ALU.add).then_inc(empty, 1)
                q, before = use_of(b, hg, use)
                dve.wait_ge(emptied[q], before + 1)
                dve.tensor_scalar(ypos[:], y[:], 0.0, None, ALU.max).then_inc(y_steps, 1)
                dve.wait_ge(y_steps, base + 1)
                dve.scalar_tensor_tensor(ypos[:], y[:], 0.0, ypos[:], ALU.min, ALU.add).then_inc(y_steps, 1)
                dve.wait_ge(y_steps, base + 2)
                dve.tensor_tensor(xs, xs, ypos[:].rearrange("p t d -> p (t d)"), ALU.add).then_inc(y_steps, 2)
                dve.wait_ge(y_steps, base + 4)

            walk(dve, dict(stats=stats, norm=norm, ln=ln, proj=proj, max=peak, maxt=maxt, vtok=vtok, ot=ot, wo=wo))


def phase_gated(nc, k, a):
    NB = S // P
    HALF = S // G
    EC = HV // P
    NBANK = 7
    BLOCKS = ((0, 0, 0), (0, 32, 1), (1, 0, 2), (1, 64, 3))

    FIRST = [(kind, r, 0) for r in range(2) for kind in ("stats", "norm")]
    BODY = [("ln", 0, h) for h in range(HALF)]
    BODY += [("proj", v, h) for h in range(HALF) for v in range(4)] + [("stats", 0, 1)]
    BODY += [("v", 0, t) for t in range(NB // 2)]
    BODY += [("gate", c, h) for c in range(EC) for h in range(HALF)]
    BODY += [("ktok", 0, h) for h in range(HALF)] + [("norm", 0, 1)] + [("att", 0, h) for h in range(HALF)]
    BODY += [("kv", 0, 0), ("stats", 1, 1)]
    BODY += [("out", c, 0) for c in range(EC)] + [("norm", 1, 1)] + [("out", c, 1) for c in range(EC)]
    BODY += [("y", 0, h) for h in range(HALF)] + [("tail", 0, 0)]
    SHARED = ("ln", "proj", "v", "gate", "ktok", "att", "out", "y")
    NBODY = sum(e[0] in SHARED for e in BODY)
    assert NBODY % NBANK == 0

    with ExitStack() as ctx:
        def sb(name, shape, dt=F32):
            return ctx.enter_context(nc.sbuf_tensor(f"gau_{name}", shape, dt))

        def sem(name):
            return ctx.enter_context(nc.semaphore(f"gau_{name}"))

        lay, _ = pack_layout()
        wqk_raw, wv_raw, wg_raw, wo_raw = (sb("wqk_raw", [P, P]), sb("wv_raw", [P, EC, P]), sb("wg_raw", [P, EC, P]),
                                           sb("wo_raw", [P, HV]))
        wqk_h, wqk_l = sb("wqk_h", [P, 4, P], F32R), sb("wqk_l", [P, 4, P], F32R)
        wv_h, wv_l = sb("wv_h", [P, HV], F32R), sb("wv_l", [P, HV], F32R)
        wg_h, wg_l = sb("wg_h", [P, HV], F32R), sb("wg_l", [P, HV], F32R)
        wo_t = sb("wo_t", [P, HV])
        par = sb("par", [P, 4, 3])
        ln1w, ln1b, bg = sb("ln1w", [P, 1]), sb("ln1b", [P, 1]), sb("bg", [P, EC])
        bv_raw, bv_row, ones = sb("bv_raw", [1, HV]), sb("bv_row", [P, HV], F32R), sb("ones", [P, P], F32R)
        bo, ln2w, ln2b = sb("bo", [P, D]), sb("ln2w", [P, D]), sb("ln2b", [P, D])
        pos, dval = sb("pos", [P, NPOS]), sb("dval", [P, NPOS])
        rel, bias, picked = sb("rel", [P, P]), sb("bias", [P, P]), sb("picked", [P, P, NPOS])
        cos, sin = sb("cos", [P, S]), sb("sin", [P, S])
        st, mv, veps, rstd = sb("st", [P, NB, 6]), sb("mv", [P, NB, 2]), sb("veps", [P, NB]), sb("rstd", [P, NB])
        xn, xn2 = sb("xn", [P, NB, D]), sb("xn2", [P, NB, D])
        xt = sb("xt", [P, 2, G])
        x_h, x_l = sb("x_h", [P, S], F32R), sb("x_l", [P, S], F32R)
        act_s, head, turned_s = sb("act_s", [P, 2, G]), sb("head", [P, 2, G]), sb("turned_s", [P, 2, G])
        stack = sb("stack", [P, 2, S])
        v_tok, gate = sb("v_tok", [P, NB, HV]), sb("gate", [P, EC, S])
        k_tok, kv = sb("k_tok", [P, NB, P]), sb("kv", [P, HV])
        att_s, att = sb("att_s", [P, 2, G]), sb("att", [P, 2, G])
        mixed = sb("mixed", [P, 2, EC, G])
        y, yn = sb("y", [P, 2, TG, D]), sb("yn", [P, 2, TG, D])
        st2, mv2, veps2, rstd2 = (sb("st2", [P, 2, TG, 6]), sb("mv2", [P, 2, TG, 2]), sb("veps2", [P, 2, TG]),
                                  sb("rstd2", [P, 2, TG]))
        flag = sb("flag", [P, 16])
        shared, kv_ps = k.banks[:, 0:NBANK, :], k.banks[:, NBANK, 0:HV]

        w_in, p_in, zeroed, turned, high_done, rel_steps = (sem(s) for s in
            ("w_in", "p_in", "zeroed", "turned", "high_done", "rel_steps"))
        params = ("L1_attn_bqk", "L1_attn_gamma", "L1_attn_beta")
        half = QK // 2
        with nc.Block() as block:
            @block.sync
            def _(sp):
                sp.wait_ge(zeroed, 1)
                sp.dma_start(wqk_raw[0:QK, :], a["L1_attn_Wqk"]).then_inc(w_in, 16)
                sp.dma_start(wv_raw[:], a["L1_attn_Wv"].rearrange("(c p) d -> p c d", p=P)).then_inc(w_in, 16)
                sp.dma_start(wg_raw[:], a["L1_attn_Wg"].rearrange("(c p) d -> p c d", p=P)).then_inc(w_in, 16)
                sp.dma_start(wo_raw[:], a["L1_attn_Wo"]).then_inc(w_in, 16)
                sp.dma_start(bv_raw[:], a["L1_attn_bv"].rearrange("(o n) -> o n", o=1)).then_inc(w_in, 16)
                for c in range(EC):
                    sp.dma_start(bg[:, c:c + 1], a["L1_attn_bg"][c * P:(c + 1) * P].rearrange("(n o) -> n o", o=1))\
                      .then_inc(w_in, 16)
                sp.dma_start(ln1w[:], a["L1_attn_ln1_w"].rearrange("(n o) -> n o", o=1)).then_inc(w_in, 16)
                sp.dma_start(ln1b[:], a["L1_attn_ln1_b"].rearrange("(n o) -> n o", o=1)).then_inc(w_in, 16)
                sp.dma_start(bo[:], a["L1_attn_bo"].partition_broadcast(P)).then_inc(w_in, 16)
                sp.dma_start(ln2w[:], a["L1_attn_ln2_w"].partition_broadcast(P)).then_inc(w_in, 16)
                sp.dma_start(ln2b[:], a["L1_attn_ln2_b"].partition_broadcast(P)).then_inc(w_in, 16)
                sp.dma_start(pos[:], a["L1_attn_pos_emb"][0:NPOS].partition_broadcast(P)).then_inc(w_in, 16)
                sp.dma_start(cos[:], a["consts"][:, slice(*lay["cos"])]).then_inc(w_in, 16)
                sp.dma_start(sin[:], a["consts"][:, slice(*lay["sin"])]).then_inc(w_in, 16)
                sp.dma_start(dval[:], a["consts"][:, slice(*lay["dval"])]).then_inc(w_in, 16)

            @block.scalar
            def _(act):
                act.wait_ge(zeroed, 1)
                n = 0
                for stk, row, which in BLOCKS:
                    for swap in range(2):
                        for c, name in enumerate(params):
                            src = a[name] if c == 0 else a[name][which]
                            for part in range(2):
                                to = row + half * (part ^ swap)
                                act.dma_start(par[to:to + half, 2 * stk + swap, c:c + 1],
                                              src[part * half:(part + 1) * half].rearrange("(n o) -> n o", o=1))\
                                   .then_inc(p_in, 16)
                                n += 1
                act.wait_ge(turned, 1)
                src = shared[:, 0, 0:QK].rearrange("p (s n) -> p s n", n=half)
                for stk, row, which in BLOCKS:
                    act.activation(wqk_h[:, 2 * stk, row:row + QK], shared[:, 0, 0:QK], ACT.Copy)
                    for part in range(2):
                        to = row + half * (1 - part)
                        act.activation(wqk_h[:, 2 * stk + 1, to:to + half], src[:, part, :], ACT.Copy)
                act.activation(wv_h[:], shared[:, 1, 0:HV], ACT.Copy)
                act.activation(wg_h[:], shared[:, 1, HV:2 * HV], ACT.Copy)
                act.activation(bv_row[0:1, :], bv_raw[:], ACT.Copy)
                act.activation(wo_t[:], shared[:, 2, 0:HV], ACT.Copy).then_inc(high_done, 1)
                act.wait_ge(p_in, 16 * n)

            @block.gpsimd
            def _(pool):
                pool.memset(wqk_raw[:], 0.0)
                pool.memset(par[:], 0.0)
                pool.memset(wqk_h[:].bitcast(F32), 0.0)
                pool.memset(wqk_l[:].bitcast(F32), 0.0)
                pool.memset(bv_row[:].bitcast(F32), 0.0).then_inc(zeroed, 1)
                pool.memset(ones[:].bitcast(F32), 1.0)
                pool.memset(kv[:], 0.0)

            @block.tensor
            def _(pe):
                pe.wait_ge(w_in, 16 * 16)
                pe.transpose(shared[:, 0, 0:P], wqk_raw[:], k.ident)
                for c in range(EC):
                    pe.transpose(shared[:, 1, c * P:(c + 1) * P], wv_raw[:, c, :], k.ident)
                    pe.transpose(shared[:, 1, HV + c * P:HV + (c + 1) * P], wg_raw[:, c, :], k.ident)
                    mm = pe.transpose(shared[:, 2, c * P:(c + 1) * P], wo_raw[:, c * P:(c + 1) * P], k.ident)
                mm.then_inc(turned, 1)

            @block.vector
            def _(dve):
                dve.wait_ge(high_done, 1)
                src = shared[:, 0, 0:QK].rearrange("p (s n) -> p s n", n=half)
                for stk, row, which in BLOCKS:
                    dve.tensor_tensor(wqk_l[:, 2 * stk, row:row + QK], shared[:, 0, 0:QK],
                                      wqk_h[:, 2 * stk, row:row + QK].bitcast(F32), ALU.subtract)
                    for part in range(2):
                        to = row + half * (1 - part)
                        dve.tensor_tensor(wqk_l[:, 2 * stk + 1, to:to + half], src[:, part, :],
                                          wqk_h[:, 2 * stk + 1, to:to + half].bitcast(F32), ALU.subtract)
                dve.tensor_tensor(wv_l[:], shared[:, 1, 0:HV], wv_h[:].bitcast(F32), ALU.subtract)
                dve.tensor_tensor(wg_l[:], shared[:, 1, HV:2 * HV], wg_h[:].bitcast(F32), ALU.subtract)
                dve.tensor_tensor(bv_row[32:33, :], bv_raw[:], bv_row[0:1, :].bitcast(F32), ALU.subtract)
                dve.wait_ge(w_in, 16 * 16)
                dve.tensor_copy(rel[:], k.const("outside")).then_inc(rel_steps, 1)
                dve.tensor_tensor(picked[:], k.const("dist").unsqueeze(2).broadcast_to([P, P, NPOS]),
                                  dval[:].unsqueeze(1).broadcast_to([P, P, NPOS]), ALU.is_equal).then_inc(rel_steps, 1)
                dve.wait_ge(rel_steps, 2)
                dve.tensor_tensor(picked[:], picked[:], pos[:].unsqueeze(1).broadcast_to([P, P, NPOS]), ALU.mult)\
                   .then_inc(rel_steps, 1)
                dve.wait_ge(rel_steps, 3)
                dve.tensor_reduce(bias[:], picked[:], AX.X, ALU.add).then_inc(rel_steps, 1)
                dve.wait_ge(rel_steps, 4)
                dve.tensor_tensor(rel[:], rel[:], bias[:], ALU.add).then_inc(rel_steps, 1)

        filled = [sem(f"filled{n}") for n in range(NBANK)]
        emptied = [sem(f"emptied{n}") for n in range(NBANK)]
        ln_steps, rstd_done, xt_done, x_h_done, x_l_done = (sem(s) for s in
            ("ln_steps", "rstd_done", "xt_done", "x_h_done", "x_l_done"))
        silu_done, rot = sem("silu_done"), sem("rot")
        kv_done, kv_out, att_steps = sem("kv_done"), sem("kv_out"), sem("att_steps")
        y_steps, rstd2_done = sem("y_steps"), sem("rstd2_done")
        LN = 4
        ROT = 5
        YS = 8

        def walk(eng, parts):
            def run(entries, b):
                use = 0
                for kind, x, z in entries:
                    if kind in parts:
                        parts[kind](b, x, z, use)
                    if kind in SHARED:
                        use += 1

            run(FIRST, 0)
            with eng.Fori(0, B - 1) as b:
                run(BODY, b)
            run([e for e in BODY if e[0] not in ("stats", "norm")], B - 1)

        def use_of(b, use):
            return use % NBANK, use // NBANK + b * (NBODY // NBANK)

        def fill(pe, b, use):
            q, before = use_of(b, use)
            pe.wait_ge(emptied[q], before + 1)
            return shared[:, q, :], filled[q]

        def content(eng, b, use):
            q, before = use_of(b, use)
            eng.wait_ge(filled[q], before + 1)
            return shared[:, q, :], emptied[q]

        def was_read(eng, b, use):
            q, before = use_of(b, use)
            eng.wait_ge(emptied[q], before + 2)

        block = ctx.enter_context(nc.Block())

        @block.tensor
        def _(pe):
            def ln(b, _, h, use):
                bank, full = fill(pe, b, use)
                pe.wait_ge(ln_steps, 2 * LN * (b + 1))
                for t in range(TG):
                    mm = pe.transpose(bank[:, t * P:(t + 1) * P], xn2[:, h * TG + t, :], k.ident)
                mm.then_inc(full, 1)

            def three(bank, full, wh, wl, h):
                pe.matmul(bank, wh, x_h[:, h * G:(h + 1) * G], start=True, stop=False)
                pe.matmul(bank, wh, x_l[:, h * G:(h + 1) * G], start=False, stop=False)
                pe.matmul(bank, wl, x_h[:, h * G:(h + 1) * G], start=False, stop=True).then_inc(full, 1)

            def proj(b, v, h, use):
                bank, full = fill(pe, b, use)
                pe.wait_ge(x_l_done, HALF * b + h + 1)
                three(bank, full, wqk_h[:, v, :], wqk_l[:, v, :], h)

            def val(b, _, t2, use):
                bank, full = fill(pe, b, use)
                for i in range(2):
                    tok = slice((2 * t2 + i) * P, (2 * t2 + i + 1) * P)
                    to = bank[:, i * HV:(i + 1) * HV]
                    pe.matmul(to, x_h[:, tok], wv_h[:], start=True, stop=False)
                    pe.matmul(to, x_l[:, tok], wv_h[:], start=False, stop=False)
                    pe.matmul(to, x_h[:, tok], wv_l[:], start=False, stop=False)
                    mm = pe.matmul(to, ones[:], bv_row[:], start=False, stop=True)
                mm.then_inc(full, 1)

            def gates(b, c, h, use):
                bank, full = fill(pe, b, use)
                three(bank, full, wg_h[:, c * P:(c + 1) * P], wg_l[:, c * P:(c + 1) * P], h)

            def ktok(b, _, h, use):
                bank, full = fill(pe, b, use)
                pe.wait_ge(rot, (HALF * 2 * b + 2 * h + 2) * ROT + ROT)
                for t in range(TG):
                    mm = pe.transpose(bank[:, t * P:(t + 1) * P], stack[:, 1, (h * TG + t) * P:(h * TG + t + 1) * P],
                                      k.ident)
                mm.then_inc(full, 1)

            def attn(b, _, h, use):
                bank, full = fill(pe, b, use)
                for t in range(TG):
                    tok = slice((h * TG + t) * P, (h * TG + t + 1) * P)
                    mm = pe.matmul(bank[:, t * P:(t + 1) * P], stack[:, 1, tok], stack[:, 0, tok], start=True,
                                   stop=True, skip_group_check=True)
                mm.then_inc(full, 1)

            def kvs(b, _, __, use):
                was_read(pe, b, use - 3)
                was_read(pe, b, use - 4)
                pe.wait_ge(kv_out, b + 1)
                for t in range(NB):
                    mm = pe.matmul(kv_ps[:], k_tok[:, t, :], v_tok[:, t, :], start=t == 0, stop=t == NB - 1)
                mm.then_inc(kv_done, 1)

            def out(b, c, h, use):
                bank, full = fill(pe, b, use)
                if h == 0 and c == 0:
                    pe.wait_ge(kv_out, b + 2)
                pe.wait_ge(att_steps, 2 * (HALF * b + h + 1))
                pe.matmul(bank, kv[:, c * P:(c + 1) * P], stack[:, 0, h * G:(h + 1) * G], start=True, stop=False,
                          skip_group_check=True)
                for t in range(TG):
                    mm = pe.matmul(bank[:, t * P:(t + 1) * P], v_tok[:, h * TG + t, c * P:(c + 1) * P],
                                   att[:, h, t * P:(t + 1) * P], start=False, stop=True, skip_group_check=True)
                mm.then_inc(full, 1)

            def ys(b, _, h, use):
                bank, full = fill(pe, b, use)
                for c in range(EC):
                    was_read(pe, b, use - HALF * EC + h * (EC - 1) + c)
                for t in range(TG):
                    for c in range(EC):
                        mm = pe.matmul(bank[:, t * P:(t + 1) * P], mixed[:, h, c, t * P:(t + 1) * P],
                                       wo_t[:, c * P:(c + 1) * P], start=t == 0 and c == 0, stop=c == EC - 1,
                                       skip_group_check=True)
                mm.then_inc(full, 1)

            walk(pe, dict(ln=ln, proj=proj, v=val, gate=gates, ktok=ktok, att=attn, kv=kvs, out=out, y=ys))

        @block.scalar
        def _(act):
            def ln(b, _, h, use):
                bank, empty = content(act, b, use)
                act.activation(xt[:, h, :], bank, ACT.Identity, bias=ln1b[:, 0:1], scale=ln1w[:, 0:1])\
                   .then_inc(empty, 1)
                was_read(act, b, use)
                act.activation(x_h[:, h * G:(h + 1) * G], xt[:, h, :], ACT.Copy).then_inc(x_h_done, 1)

            def proj(b, v, h, use):
                bank, empty = content(act, b, use)
                act.wait_ge(rot, (HALF * 2 * b + 2 * h + v // 2) * ROT + 1 + v % 2)
                act.activation(act_s[:, v % 2, :], bank, ACT.Silu, bias=par[:, v, 0:1]).then_inc(empty, 1)

            def val(b, _, t2, use):
                bank, empty = content(act, b, use)
                act.activation(v_tok[:, 2 * t2:2 * t2 + 2, :], bank.rearrange("p (t e) -> p t e", t=2), ACT.Silu)\
                   .then_inc(empty, 1)

            def gates(b, c, h, use):
                bank, empty = content(act, b, use)
                act.activation(gate[:, c, h * G:(h + 1) * G], bank, ACT.Silu, bias=bg[:, c:c + 1]).then_inc(empty, 1)

            def ktok(b, _, h, use):
                bank, empty = content(act, b, use)
                act.activation(k_tok[:, h * TG:(h + 1) * TG, :], bank.rearrange("p (t r) -> p t r", t=TG), ACT.Copy)\
                   .then_inc(empty, 1)

            def kvs(b, _, __, use):
                act.wait_ge(kv_done, b + 1)
                act.activation(kv[32:64, :], kv_ps[64:96, :], ACT.Copy, scale=1.0 / S).then_inc(kv_out, 1)

            act.activation(kv[0:1, 0:1], k.const("qlow")[0:1, :], ACT.Copy).then_inc(kv_out, 1)
            walk(act, dict(ln=ln, proj=proj, v=val, gate=gates, ktok=ktok, kv=kvs))

        @block.gpsimd
        def _(pool):
            def norm(b, r, ahead, use):
                n = 2 * (b + ahead) + r
                pool.wait_ge(ln_steps, n * LN + 3)
                pool.tensor_tensor(rstd[:], veps[:], k.neghalf[:, 0:NB], ALU.pow).then_inc(rstd_done, 1)

            def tail(b, _, __, use):
                pool.wait_ge(y_steps, b * YS + 3)
                pool.tensor_tensor(rstd2[:], veps2[:], k.neghalf[:, 0:NB].rearrange("p (h t) -> p h t", t=TG), ALU.pow).then_inc(rstd2_done, 1)

            walk(pool, dict(norm=norm, tail=tail))

        @block.vector
        def _(dve):
            def src(b, r, t):
                return k.x[:, bass.ds(b * S + t * P, P)] if r == 0 else xn[:, t, :]

            def stats(b, r, ahead, use):
                n = 2 * (b + ahead) + r
                for t in range(NB):
                    ins = dve.bn_stats(st[:, t, :], src(b + ahead, r, t))
                ins.then_inc(ln_steps, 1)
                dve.wait_ge(ln_steps, n * LN + 1)
                pause(dve, k)
                for t in range(NB):
                    ins = dve.bn_aggr(mv[:, t, :], st[:, t, :])
                ins.then_inc(ln_steps, 1)
                dve.wait_ge(ln_steps, n * LN + 2)
                dve.tensor_scalar(veps[:], mv[:, :, 1], EPS, None, ALU.add).then_inc(ln_steps, 1)

            def norm(b, r, ahead, use):
                n = 2 * (b + ahead) + r
                dve.wait_ge(rstd_done, n + 1)
                for t in range(NB):
                    ins = dve.tensor_scalar((xn, xn2)[r][:, t, :], src(b + ahead, r, t), mv[:, t, 0:1],
                                            rstd[:, t:t + 1], ALU.subtract, ALU.mult)
                ins.then_inc(ln_steps, 1)
                dve.wait_ge(ln_steps, n * LN + 4)

            def ln(b, _, h, use):
                dve.wait_ge(x_h_done, HALF * b + h + 1)
                dve.tensor_tensor(x_l[:, h * G:(h + 1) * G], xt[:, h, :], x_h[:, h * G:(h + 1) * G].bitcast(F32),
                                  ALU.subtract).then_inc(x_l_done, 1)

            def proj(b, v, h, use):
                base = (HALF * 2 * b + 2 * h + v // 2 + 1) * ROT
                was_read(dve, b, use)
                q = v % 2
                dve.tensor_scalar(head[:, q, :], act_s[:, q, :], par[:, v, 1:2], par[:, v, 2:3], ALU.mult, ALU.add)\
                   .then_inc(rot, 1)
                if q == 0:
                    return
                cut = slice(h * G, (h + 1) * G)
                dve.wait_ge(rot, base + 1)
                dve.tensor_tensor(turned_s[:, 0, :], head[:, 0, :], cos[:, cut], ALU.mult).then_inc(rot, 1)
                dve.wait_ge(rot, base + 2)
                dve.tensor_tensor(turned_s[:, 1, :], head[:, 1, :], sin[:, cut], ALU.mult).then_inc(rot, 1)
                dve.wait_ge(rot, base + 4)
                dve.tensor_tensor(stack[:, v // 2, cut], turned_s[:, 0, :], turned_s[:, 1, :], ALU.add).then_inc(rot, 1)
                dve.wait_ge(rot, base + 5)

            def attn(b, _, h, use):
                bank, empty = content(dve, b, use)
                dve.scalar_tensor_tensor(att_s[:, h, :].rearrange("p (t i) -> p t i", t=TG),
                                         bank.rearrange("p (t i) -> p t i", t=TG), 1.0 / SPAN,
                                         rel[:].unsqueeze(1).broadcast_to([P, TG, P]), ALU.mult, ALU.add)\
                   .then_inc(empty, 1)
                was_read(dve, b, use)
                dve.scalar_tensor_tensor(att[:, h, :], att_s[:, h, :], 0.0, att_s[:, h, :], ALU.max, ALU.mult)\
                   .then_inc(att_steps, 2)

            def out(b, c, h, use):
                bank, empty = content(dve, b, use)
                dve.tensor_tensor(mixed[:, h, c, :], bank, gate[:, c, h * G:(h + 1) * G], ALU.mult).then_inc(empty, 1)

            def ys(b, _, h, use):
                bank, empty = content(dve, b, use)
                dve.tensor_tensor(y[:, h], bank.rearrange("p (t d) -> p t d", d=D),
                                  bo[:].unsqueeze(1).broadcast_to([P, TG, D]), ALU.add).then_inc(empty, 1)

            def tail(b, _, __, use):
                base = b * YS
                y8, yn8 = (v[:].rearrange("p h t d -> p (h t) d") for v in (y, yn))
                mv8, rstd8 = mv2[:].rearrange("p h t c -> p (h t) c"), rstd2[:].rearrange("p h t -> p (h t)")

                def wide(v):
                    return v[:].unsqueeze(1).broadcast_to([P, NB, D])

                for h in range(HALF):
                    was_read(dve, b, use - HALF + h)
                for t in range(NB):
                    ins = dve.bn_stats(st2[:, t // TG, t % TG, :], y8[:, t, :])
                ins.then_inc(y_steps, 1)
                dve.wait_ge(y_steps, base + 1)
                pause(dve, k)
                for t in range(NB):
                    ins = dve.bn_aggr(mv8[:, t, :], st2[:, t // TG, t % TG, :])
                ins.then_inc(y_steps, 1)
                dve.wait_ge(y_steps, base + 2)
                dve.tensor_scalar(veps2[:].rearrange("p h t -> p (h t)"), mv8[:, :, 1], EPS, None, ALU.add)\
                   .then_inc(y_steps, 1)
                dve.wait_ge(rstd2_done, b + 1)
                for t in range(NB):
                    ins = dve.tensor_scalar(yn8[:, t, :], y8[:, t, :], mv8[:, t, 0:1], rstd8[:, t:t + 1],
                                            ALU.subtract, ALU.mult)
                ins.then_inc(y_steps, 1)
                dve.wait_ge(y_steps, base + 4)
                dve.tensor_tensor(y8, yn8, wide(ln2w), ALU.mult).then_inc(y_steps, 1)
                dve.wait_ge(y_steps, base + 5)
                dve.tensor_tensor(yn8, y8, wide(ln2b), ALU.add).then_inc(y_steps, 1)
                dve.wait_ge(y_steps, base + 6)
                xs = k.x[:, bass.ds(b * S, S)].rearrange("p (t d) -> p t d", d=D)
                dve.tensor_tensor(xs, xs, yn8, ALU.add).then_inc(y_steps, YS - 6)
                dve.wait_ge(y_steps, base + YS)

            for q in range(NBANK):
                dve.tensor_copy(flag[:, 2 + q:3 + q], k.ident[:, 0:1]).then_inc(emptied[q], 1)
            dve.tensor_copy(flag[:, 2 + NBANK:3 + NBANK], k.ident[:, 0:1]).then_inc(rot, ROT)
            walk(dve, dict(stats=stats, norm=norm, ln=ln, proj=proj, att=attn, out=out, y=ys, tail=tail))


def phase_store(nc, k, out):
    with ExitStack() as ctx:
        stored = ctx.enter_context(nc.semaphore("stored"))
        block = ctx.enter_context(nc.Block())

        @block.sync
        def _(sp):
            sp.dma_start(out.rearrange("b (n p) d -> p (b n) d", p=P),
                         k.x[:].rearrange("p (n d) -> p n d", d=D)).then_inc(stored, 16)
            sp.wait_ge(stored, 16)


def build(nc, a, out, phases=("ffn0a", "att", "ffn0b", "ffn1a", "gau", "ffn1b")):
    k = Core()
    lay, npack = pack_layout()
    with ExitStack() as ctx:
        def sb(name, shape, dt=F32):
            return ctx.enter_context(nc.sbuf_tensor(name, shape, dt))

        k.x = sb("x", [P, NT * D])
        k.pack = sb("pack", [P, lay["sel0"][0]])
        k.const = lambda name: k.pack[:, lay[name][0]:lay[name][1]]
        k.ident = k.const("ident")
        k.rth, k.rtl = sb("rth", [P, P], F32R), sb("rtl", [P, P], F32R)
        k.gate_bias = sb("gate_bias", [P, E0])
        k.neghalf = sb("neghalf", [P, 8])
        k.banks = ctx.enter_context(nc.psum_tensor("banks", [P, 8, 512], F32))
        k.unread = sb("unread", [P, 1])
        for layer in range(2):
            with ExitStack() as own:
                NC, NSEL = (C0, C0) if layer == 0 else (C1, E1)

                def ws(name, n, dt=F32R):
                    return own.enter_context(nc.sbuf_tensor(f"{name}{layer}", [P, n * P], dt))

                k.wgh, k.wgl, k.wuh, k.wul = ws("wgh", NC), ws("wgl", NC), ws("wuh", NC), ws("wul", NC)
                k.wdh, k.wdl, k.sel = ws("wdh", NC), ws("wdl", NC), ws("sel", NSEL)
                phase_setup(nc, k, a, layer)
                k.moe_sems, k.for_layer, turns = {}, own.enter_context, 0
                for name in (("ffn0a", "att", "ffn0b"), ("ffn1a", "gau", "ffn1b"))[layer]:
                    if name not in phases:
                        continue
                    if name == "att":
                        phase_attention(nc, k, a)
                    elif name == "gau":
                        phase_gated(nc, k, a)
                    else:
                        phase_moe(nc, k, name, layer, turns)
                        turns += 1
        phase_store(nc, k, out)


_INS = ['L0_attn_x', 'L0_attn_w_in', 'L0_attn_b_in', 'L0_attn_w_out', 'L0_attn_b_out', 'L0_ffn_gate_w',
        'L0_ffn_gate_bias', 'L0_ffn_w1', 'L0_ffn_w2', 'L0_ffn_w3', 'L0_ffn_ws1', 'L0_ffn_ws2', 'L0_ffn_ws3',
        'L1_attn_ln1_w', 'L1_attn_ln1_b', 'L1_attn_Wqk', 'L1_attn_bqk', 'L1_attn_Wv', 'L1_attn_bv', 'L1_attn_Wg',
        'L1_attn_bg', 'L1_attn_Wo', 'L1_attn_bo', 'L1_attn_ln2_w', 'L1_attn_ln2_b', 'L1_attn_gamma',
        'L1_attn_beta', 'L1_attn_pos_emb', 'L1_ffn_router_w', 'L1_ffn_w_gate', 'L1_ffn_w_up', 'L1_ffn_w_down']


def kernel(**inputs):
    import numpy as _np
    import concourse.bacc as _bacc
    from concourse import mybir as _mybir
    from concourse.bass_utils import run_bass_kernel_spmd as _run

    nc = _bacc.Bacc("TRN2", target_bir_lowering=False, num_devices=1)
    arrays, args = {}, {}
    for name in _INS + ["consts"]:
        x = constants() if name == "consts" else _np.ascontiguousarray(inputs[name])
        arrays[f"in_{name}_dram"] = x
        args[name] = nc.dram_tensor(f"in_{name}_dram", x.shape, _mybir.dt.from_np(x.dtype), kind="ExternalInput").ap()
    out = nc.dram_tensor("out_0_dram", (B, S, D), _mybir.dt.float32, kind="ExternalOutput").ap()
    build(nc, args, out)
    r = _run(nc, [arrays], core_ids=[0])
    return r.results[0]["out_0_dram"]
```
